# Optimizing a Trainium2 kernel written in Bass

```python
import numpy as np
import jax
import jax.numpy as jnp

def _softmax(x, axis=-1):
    return jax.nn.softmax(x, axis=axis)

def _gelu(x):
    return jax.nn.gelu(x, approximate=True)

def _silu(x):
    return jax.nn.silu(x)

def _sigmoid(x):
    return jax.nn.sigmoid(x)

def _layernorm(x, axis=-1, eps=1e-05):
    m = jnp.mean(x, axis=axis, keepdims=True)
    v = jnp.var(x, axis=axis, keepdims=True)
    return (x - m) / jnp.sqrt(v + eps)

def _scatter_add(tgt, idx, src, axis=0):
    return tgt.at[idx].add(src)

def _segment_sum(src, seg, n):
    return jax.ops.segment_sum(src, seg, n)
kernel_name = 'mk_flamingo_gated_d1_seqx_r8_219156'

def setup_inputs(seed: int=0):
    np.random.seed(seed)
    _w = jnp.asarray

    def _rec_inputs():
        import jax
        import jax.numpy as jnp
        _rk = jax.random.key(seed)
        x = 7.22e-05 + 1 * jax.random.normal(jax.random.fold_in(_rk, 1), (16, 128, 256), jnp.float32)
        _lenS = 128 - jax.random.randint(jax.random.fold_in(_rk, 7), (16,), 0, max(1, 128 // 4) + 1, jnp.int32)
        _lenS2 = 128 - jax.random.randint(jax.random.fold_in(_rk, 8), (16,), 0, max(1, 128 // 4) + 1, jnp.int32)
        _ctx_2048P = jax.random.normal(jax.random.fold_in(_rk, 11), (16, 16, 256), jnp.float32)
        _ctx_2048c = jax.random.dirichlet(jax.random.fold_in(_rk, 511), 0.3 * jnp.ones((16,), jnp.float32), (16, 128))
        _ctx_2048t = jnp.einsum('bsk,bkd->bsd', _ctx_2048c, _ctx_2048P)
        _ctx_2048t = _ctx_2048t * jax.lax.rsqrt(jnp.mean(jnp.square(_ctx_2048t)) + 1e-12) * 0.953939
        ctx_2048 = 4.13588e-05 + 0.999923 * (_ctx_2048t + 0.3 * jax.random.normal(jax.random.fold_in(_rk, 611), (16, 128, 256), jnp.float32))
        _g = jax.random.normal(jax.random.fold_in(_rk, 9001), (2, 1), jnp.float32)
        _g = jnp.sign(_g) * jnp.maximum(jnp.abs(_g), 1.0) + (_g == 0) * 1.0
        g_xattn = _g[0]
        g_ffn = _g[1]
        return (x, ctx_2048, g_xattn, g_ffn)
    x, ctx_2048, g_xattn, g_ffn = _rec_inputs()

    def _L0_xattn_setup():
        import jax, jax.numpy as jnp
        import numpy as np
        N_HEAD = 8
        key = jax.random.key(seed)
        k1, k2, k3 = jax.random.split(key, 3)
        B, D, L = (4, 128, 256)
        q = jax.random.normal(k1, (B, D, L), dtype=jnp.float32)
        k = jax.random.normal(k2, (B, D, L), dtype=jnp.float32)
        v = jax.random.normal(k3, (B, D, L), dtype=jnp.float32)
        gamma = jnp.ones((), dtype=jnp.float32)
        return {'q': q, 'k': k, 'v': v, 'gamma': gamma}
    _L0_xattn_all = _L0_xattn_setup()
    _L0_xattn_in = {k: v for k, v in _L0_xattn_all.items() if k in ('gamma',)}
    del _L0_xattn_all

    def _L0_ffn_setup():
        import jax, jax.numpy as jnp
        import numpy as np
        B, S, H, I = (1, 64, 256, 768)

        def _quantized_matmul(x, w, scale):
            wq = w.astype(jnp.float8_e4m3fn).astype(x.dtype)
            y = jnp.einsum('bsi,io->bso', x, wq)
            return y * scale
        key = jax.random.key(seed)
        ks = jax.random.split(key, 7)
        return {'x': jax.random.normal(ks[0], (B, S, H), dtype=jnp.float32), 'gate_w': jax.random.normal(ks[1], (H, I), dtype=jnp.float32) * 0.02, 'up_w': jax.random.normal(ks[2], (H, I), dtype=jnp.float32) * 0.02, 'down_w': jax.random.normal(ks[3], (I, H), dtype=jnp.float32) * 0.02, 'gate_scale': jax.random.uniform(ks[4], (I,), dtype=jnp.float32, minval=0.5, maxval=1.5), 'up_scale': jax.random.uniform(ks[5], (I,), dtype=jnp.float32, minval=0.5, maxval=1.5), 'down_scale': jax.random.uniform(ks[6], (H,), dtype=jnp.float32, minval=0.5, maxval=1.5)}
    _L0_ffn_all = _L0_ffn_setup()
    _L0_ffn_in = {k: v for k, v in _L0_ffn_all.items() if k in ('gate_w', 'up_w', 'down_w', 'gate_scale', 'up_scale', 'down_scale')}
    del _L0_ffn_all
    return {'x': x, 'ctx_2048': ctx_2048, 'g_xattn': g_xattn, 'g_ffn': g_ffn, 'L0_xattn_gamma': _L0_xattn_in['gamma'], 'L0_ffn_gate_w': _L0_ffn_in['gate_w'], 'L0_ffn_up_w': _L0_ffn_in['up_w'], 'L0_ffn_down_w': _L0_ffn_in['down_w'], 'L0_ffn_gate_scale': _L0_ffn_in['gate_scale'], 'L0_ffn_up_scale': _L0_ffn_in['up_scale'], 'L0_ffn_down_scale': _L0_ffn_in['down_scale']}

def reference(x, ctx_2048, g_xattn, g_ffn, L0_xattn_gamma, L0_ffn_gate_w, L0_ffn_up_w, L0_ffn_down_w, L0_ffn_gate_scale, L0_ffn_up_scale, L0_ffn_down_scale):
    import jax
    import jax.numpy as jnp

    def _L0_xattn_ref(q, k, v, gamma):
        import jax, jax.numpy as jnp
        import numpy as np
        N_HEAD = 8
        B, Dq, Lq = q.shape
        Dv, Lk = (v.shape[-2], v.shape[-1])
        h = N_HEAD
        dq = Dq // h
        dv = Dv // h
        qh = q.reshape(B, h, dq, Lq)
        kh = k.reshape(B, h, dq, Lk)
        vh = v.reshape(B, h, dv, Lk)
        scale = 1.0 / jnp.sqrt(jnp.asarray(dq, dtype=q.dtype))
        qk = jnp.einsum('bhdq,bhdl->bhql', qh, kh) * scale
        sm = jax.nn.softmax(qk, axis=-1)
        ret = jnp.einsum('bhql,bhdl->bhdq', sm, vh)
        ret = ret.reshape(B, Dv, Lq)
        return gamma * ret

    def _L0_ffn_ref(x, gate_w, up_w, down_w, gate_scale, up_scale, down_scale):
        import jax, jax.numpy as jnp
        import numpy as np
        B, S, H, I = (1, 64, 256, 768)

        def _quantized_matmul(x, w, scale):
            wq = w.astype(jnp.float8_e4m3fn).astype(x.dtype)
            y = jnp.einsum('bsi,io->bso', x, wq)
            return y * scale
        gate = jax.nn.silu(_quantized_matmul(x, gate_w, gate_scale))
        up = _quantized_matmul(x, up_w, up_scale)
        fuse = gate * up
        return _quantized_matmul(fuse, down_w, down_scale)
    x = x + jnp.tanh(g_xattn[0]) * _L0_xattn_ref(_layernorm(x, axis=-1), ctx_2048, ctx_2048, L0_xattn_gamma)
    x = x + jnp.tanh(g_ffn[0]) * _L0_ffn_ref(_layernorm(x, axis=-1), L0_ffn_gate_w, L0_ffn_up_w, L0_ffn_down_w, L0_ffn_gate_scale, L0_ffn_up_scale, L0_ffn_down_scale)
    return x

_drawn_inputs = setup_inputs


def setup_inputs(seed=0):
    import zlib

    import numpy as np

    out = dict(_drawn_inputs(seed))
    spreads = {}
    factors = {'L0_ffn_gate_scale': 6.804, 'L0_ffn_up_scale': 7.887, 'L0_ffn_down_scale': 7.643}
    for name, (base, spread) in spreads.items():
        noise = np.random.default_rng([zlib.crc32(name.encode()), seed]).standard_normal(out[name].shape)
        drawn = base * np.exp(spread * noise) if base else spread * noise
        out[name] = jnp.asarray(drawn.astype(out[name].dtype))
    for name, factor in factors.items():
        out[name] = (out[name] * factor).astype(out[name].dtype)
    return out
```

```python
import concourse.bass as bass
from concourse import mybir
from contextlib import ExitStack

NB = 16
D = 128
L = 256
NH = 8
DH = D // NH
P = 128
LT = L // P
NPART = 3
Q_PART = [0, 0, 0, 1, 1, 2]
K_PART = [0, 1, 2, 0, 1, 0]
KS = DH * len(Q_PART)
MAXROWS = 2
RING = 4
QUAD = 4
SLOTW = 32
I = 768
IT = I // P
HT = L // P
CH = 4
NCH = NB // CH
TOK = CH * P
EPS = 1e-5
E4M3_MIN_EXP = 2.0 ** -6
E4M3_MAGIC = 1.5 * 2.0 ** 20


def build(nc, x, ctx, g_xattn, g_ffn, gamma, gate_w, up_w, down_w, gate_scale, up_scale, down_scale, out):
    f32, f32r, bf16, f16, u32 = (mybir.dt.float32, mybir.dt.float32r, mybir.dt.bfloat16,
                                 mybir.dt.float16, mybir.dt.uint32)
    ALU = mybir.AluOpType
    ACT = mybir.ActivationFunctionType
    AX = mybir.AxisListType

    es = ExitStack()
    with es:
        def sb(name, shape, dt=f32):
            return es.enter_context(nc.sbuf_tensor(name, shape, dt))

        def sem(name):
            return es.enter_context(nc.semaphore(name))

        def sems(name, n=RING):
            return [sem(f"{name}{j}") for j in range(n)]

        q_scr = nc.dram_tensor("q_scr", (NB, NPART, DH, NH, L), bf16, kind="Internal").ap()
        k_scr = nc.dram_tensor("k_scr", (NB, NPART, DH, NH, L), bf16, kind="Internal").ap()
        s_scr = nc.dram_tensor("s_scr", (NB, NH, L), f32, kind="Internal").ap()
        r_scr = nc.dram_tensor("r_scr", (NB, NH, L), f32, kind="Internal").ap()

        ident = sb("ident", [P, P])
        x_sb = sb("x_sb", [P, NB, L])
        ctx_t = sb("ctx_t", [P, RING, L])
        xn = sb("xn", [P, 2, L])
        rest = sb("rest", [P, L])
        rest_v = sb("rest_v", [P, L])
        q_parts = sb("q_parts", [P, 2, NPART, L], bf16)
        k_parts = sb("k_parts", [P, 2, NPART, L], bf16)
        q_st = sb("q_st", [P, RING, NH, L], bf16)
        k_st = sb("k_st", [P, RING, NH, L], bf16)
        neg_max = sb("neg_max", [P, 2, QUAD * LT])
        max_t = sb("max_t", [QUAD * LT, 2, MAXROWS, P], bf16)
        p_t = sb("p_t", [P, 2, NH, LT * L])
        v_t = sb("v_t", [P, 2, LT, NH, SLOTW])
        u_sb = sb("u_sb", [P, 2, 2, L])
        s_sp = sb("s_sp", [P, RING, NH * L // P])
        r_sp = sb("r_sp", [P, RING, NH * L // P])
        u_n = sb("u_n", [P, RING, L])
        r_n = sb("r_n", [P, RING, L])
        a_n = sb("a_n", [P, 2, L])
        stats = sb("stats", [P, NB, 6])
        mv = sb("mv", [P, NB, 2])
        veps = sb("veps", [P, NB])
        rstd = sb("rstd", [P, NB])
        mhalf = sb("mhalf", [P, NB])
        gates = sb("gates", [P, 3])
        tanhs = sb("tanhs", [P, 2])
        c_att = sb("c_att", [P, 1])
        gs = sb("gs", [P, IT])
        us = sb("us", [P, IT])
        gs_half = sb("gs_half", [P, IT])
        gus = sb("gus", [P, IT])
        ds_row = sb("ds_row", [P, L])
        w_raw = [sb("wg_raw", [P, HT, I]), sb("wu_raw", [P, HT, I]), sb("wd_raw", [P, IT, L])]
        w_exp = [sb(f"w_exp{m}", [P, HT * I]) for m in range(2)]
        wg = sb("wg", [P, HT, I], f16)
        wu = sb("wu", [P, HT, I], f16)
        wd = sb("wd", [P, IT, L], f32r)
        xn2 = sb("xn2", [P, CH, L])
        x_t = sb("x_t", [P, 2, HT, TOK], f16)
        th, ga, fu = (p_t[:, 0, 2 * m:2 * m + 2, :] for m in range(3))
        f_hi = sb("f_hi", [P, IT, TOK], f32r)
        f_lo = sb("f_lo", [P, IT, TOK], f32r)
        yo = sb("yo", [P, 2, L])
        o_sb = sb("o_sb", [P, 2, L])
        ps = es.enter_context(nc.psum_tensor("ps", [P, 8, 512], f32))
        PS_S, PS_ST, PS_U, PS_M = 0, 2, 6, 7
        PS_GU, PS_T, PS_Y = 0, 4, 6

        x_in = sems("x_in", 5)
        ctx_in = sems("ctx_in")
        gates_in = sem("gates_in")
        scales_in = sem("scales_in")
        w_in = sem("w_in")
        consts = sem("consts")
        ones_set = sem("ones_set")
        veps_ok = sem("veps_ok")
        rstd_ok = sem("rstd_ok")
        tanh_ok = sem("tanh_ok")
        coef_ok = sem("coef_ok")
        xn_ok = sem("xn_ok")
        q_split = sem("q_split")
        k_split = sem("k_split")
        pre_split = sem("pre_split")
        scr_out = sems("scr_out")
        st_in = sems("st_in")
        mx_in = [sems(f"mx_in{q}_") for q in range(2)]
        s_ok = sem("s_ok")
        max_ok = sem("max_ok")
        mt_ok = sem("mt_ok")
        mt_hi = sem("mt_hi")
        mt_split = sem("mt_split")
        st_ok = sem("st_ok")
        exp_ok = sem("exp_ok")
        vt_ok = sem("vt_ok")
        vt_sb = sem("vt_sb")
        pv_ok = sem("pv_ok")
        u_ok = sem("u_ok")
        u_in = sems("u_in")
        sum_out = sems("sum_out")
        sum_in = sems("sum_in")
        rec_ok = sem("rec_ok")
        rec_out = sems("rec_out")
        rec_in = sems("rec_in")
        att_ok = sem("att_ok")
        x1_ok = sem("x1_ok")
        dve = sem("dve_order")
        pool_o = sem("pool_order")
        taken = sems("taken", 2)
        w_exp_ok = sem("w_exp_ok")
        w_ok = sem("w_ok")
        v2_ok = sem("v2_ok")
        r2_ok = sem("r2_ok")
        n2_ok = sem("n2_ok")
        t_ok = sem("t_ok")
        hi_ok = sem("hi_ok")
        lo_ok = sem("lo_ok")
        gu_ok = sem("gu_ok")
        th_ok = sem("th_ok")
        fu_ok = sem("fu_ok")
        fh_ok = sem("fh_ok")
        fl_ok = sem("fl_ok")
        y_ok = sem("y_ok")
        o_ok = sem("o_ok")
        out_ok = sems("out_ok", 2)
        n2_stats = sem("n2_stats")
        n2_aggr = sem("n2_aggr")
        ga_ok = sem("ga_ok")
        yo_ok = sem("yo_ok")

        block = es.enter_context(nc.Block())

        def has(i, k, off):
            return not isinstance(i, int) or 0 <= RING * i + k + off < NB

        def apart(eng, which):
            eng.sem_inc(taken[which], 1)

        def final(i):
            return isinstance(i, int) and i == NB // RING - 1

        def rs(i, k, off):
            return i + (k + off) // RING, (k + off) % RING

        def steps(eng, step):
            for k in range(RING):
                step(0, k)
            with eng.Fori(1, NB // RING - 1) as i:
                for k in range(RING):
                    step(i, k)
            for k in range(RING):
                step(NB // RING - 1, k)
            for k in range(3):
                step(NB // RING, k)

        x_piece = [0, 1, 2, 2] + [3] * 4 + [4] * 8
        pieces = [(0, 1), (1, 2), (2, 4), (4, 8), (8, 16)]

        @block.sync
        def _(sp):
            def load_ctx(b, slot):
                sp.dma_start(ctx_t[:, slot, :], ctx[b]).then_inc(ctx_in[slot], 16)

            def load_x(n):
                lo, hi = pieces[n]
                sp.dma_start(x_sb[:, lo:hi, :], x[lo:hi].rearrange("b p l -> p b l")).then_inc(x_in[n], 16)

            def save_parts(i, k, off):
                r, s = rs(i, k, off)
                b = RING * r + s
                for parts, scr in ((q_parts, q_scr), (k_parts, k_scr)):
                    for part in range(NPART):
                        dst = scr[bass.ds(b, 1), part].rearrange("a d h l -> h (a d) l")
                        sp.dma_start(dst, parts[:, s % 2, part, :]).then_inc(scr_out[s], 16)

            def load_stacks(i, k, off):
                r, s = rs(i, k, off)
                b = RING * r + s
                sp.wait_ge(scr_out[s], 96 * (r + 1))
                for c, part in enumerate(Q_PART):
                    src = q_scr[bass.ds(b, 1), part].rearrange("a d h l -> (a d) h l")
                    sp.dma_start(q_st[DH * c:DH * (c + 1), s], src).then_inc(st_in[s], 16)
                row = 0
                for n in (3, 2, 1):
                    src = k_scr[bass.ds(b, 1), 0:n].rearrange("a c d h l -> (a c d) h l")
                    sp.dma_start(k_st[row:row + n * DH, s], src).then_inc(st_in[s], 16)
                    row += n * DH

            def load_maxima(i, k, off, quad):
                r, s = rs(i, k, off)
                sp.wait_ge(mt_split, 2 * (RING * r + s) + quad + 1)
                for part in range(MAXROWS):
                    dst = q_st[KS + part:KS + part + 1, s, QUAD * quad:QUAD * (quad + 1)]
                    sp.dma_start(dst.rearrange("p h l -> p (h l)"),
                                 max_t[:, quad, part, :]).then_inc(mx_in[quad][s], 16)

            load_x(0)
            load_ctx(0, 0)
            load_x(1)
            load_ctx(1, 1)
            for dst, src in ((gates[:, 0:1], g_xattn), (gates[:, 1:2], g_ffn), (gates[:, 2:3], gamma)):
                sp.dma_start(dst, src.rearrange("(a c) -> a c", c=1).broadcast_to([P, 1])).then_inc(gates_in, 16)
            load_x(2)
            load_ctx(2, 2)
            load_ctx(3, 3)
            for b in range(2):
                sp.wait_ge(pre_split, b + 1)
                save_parts(0, b, 0)
                load_stacks(0, b, 0)
            load_x(3)
            load_x(4)
            sp.dma_start(gs[:], gate_scale.rearrange("(t p) -> p t", p=P), allow_slow_non_contiguous=True).then_inc(scales_in, 16)
            sp.dma_start(us[:], up_scale.rearrange("(t p) -> p t", p=P), allow_slow_non_contiguous=True).then_inc(scales_in, 16)
            sp.dma_start(ds_row[:], down_scale.rearrange("(a c) -> a c", a=1).broadcast_to([P, L])).then_inc(scales_in, 16)
            for b in range(2, RING):
                sp.wait_ge(q_split, b - 1)
                sp.wait_ge(k_split, b - 1)
                save_parts(0, b, 0)
                if b == 2:
                    load_stacks(0, b, 0)
            load_maxima(0, 0, 0, 0)
            load_maxima(0, 0, 0, 1)
            for dst, src in ((w_raw[0], gate_w), (w_raw[1], up_w), (w_raw[2], down_w)):
                sp.dma_start(dst[:], src.rearrange("(t p) n -> p t n", p=P)).then_inc(w_in, 16)

            def step(i, k):
                b = RING * i + k
                if has(i, k, 1):
                    load_maxima(i, k, 1, 0)
                if has(i, k, -1):
                    r, s = rs(i, k, -1)
                    sp.wait_ge(u_ok, b)
                    src = u_sb[:, s % 2]
                    for j in range(QUAD):
                        for half in range(2):
                            h = QUAD * half + j
                            sp.dma_start(u_n[DH * h:DH * (h + 1), s, :],
                                         src[32 * j + 1:32 * j + 1 + DH, half, :]).then_inc(u_in[s], 16)
                        sp.dma_start(s_scr[bass.ds(b - 1, 1)].rearrange("a (f j) l -> (a j) f l", j=QUAD)[j:j + 1],
                                     src[32 * j:32 * j + 1]).then_inc(sum_out[s], 16)
                if has(i, k, 4):
                    sp.wait_ge(vt_ok, b + 1)
                    if not isinstance(i, int) or b >= 2:
                        sp.wait_ge(k_split, b - 1)
                    sp.dma_start(ctx_t[:, k, :], ctx[bass.ds(b + 4, 1)].rearrange("a p l -> (a p) l")
                                 ).then_inc(ctx_in[k], 16)
                if has(i, k, 3):
                    if has(i, k, -1):
                        sp.wait_ge(st_ok, 4 * b)
                    load_stacks(i, k, 3)
                if has(i, k, -2):
                    r, s = rs(i, k, -2)
                    sp.wait_ge(rec_ok, b - 1)
                    sp.dma_start(r_scr[bass.ds(b - 2, 1)].rearrange("a h (c w) -> (a h c) w", w=NH * L // P),
                                 r_sp[:, s, :]).then_inc(rec_out[s], 16)
                if has(i, k, 1):
                    load_maxima(i, k, 1, 1)
                if has(i, k, -1):
                    r, s = rs(i, k, -1)
                    sp.wait_ge(sum_out[s], 64 * (r + 1))
                    sp.dma_start(s_sp[:, s, :], s_scr[bass.ds(b - 1, 1)].rearrange("a h (c w) -> (a h c) w", w=NH * L // P)
                                 ).then_inc(sum_in[s], 16)
                if has(i, k, -2):
                    r, s = rs(i, k, -2)
                    sp.wait_ge(rec_out[s], 16 * (r + 1))
                    for h in range(NH):
                        sp.dma_start(r_n[DH * h:DH * (h + 1), s, :],
                                     r_scr[bass.ds(b - 2, 1), h].broadcast_to([DH, L])).then_inc(rec_in[s], 16)
                if has(i, k, 4):
                    sp.wait_ge(q_split, b + 3)
                    sp.wait_ge(k_split, b + 3)
                    save_parts(i, k, 4)

            steps(sp, step)

            def store(b, n):
                sp.wait_ge(o_ok, b + 1)
                sp.dma_start(out[bass.ds(b, 1)].rearrange("a p l -> (a p) l"), o_sb[:, n, :]).then_inc(out_ok[n], 16)

            with sp.Fori(0, NB // 2) as j:
                for n in range(2):
                    store(2 * j + n, n)
            for n in range(2):
                sp.wait_ge(out_ok[n], 16 * (NB // 2))

        @block.gpsimd
        def _(pool):
            n_pool = [0]

            def link(ins):
                n_pool[0] += 1
                ins.then_inc(pool_o, 1)
                pool.wait_ge(pool_o, n_pool[0])

            link(nc.gpsimd.memset(ident[:], 0.0))
            nc.gpsimd.affine_select(out=ident[:], in_=ident[:], compare_op=ALU.not_equal, fill=1.0, base=0,
                                    pattern=[[-1, P]], channel_multiplier=1).then_inc(consts, 1)
            nc.gpsimd.memset(mhalf[:], -0.5).then_inc(consts, 1)
            pool.wait_ge(consts, 2)
            for n in range(len(pieces)):
                lo, hi = pieces[n]
                if n == 2:
                    pool.wait_ge(rstd_ok, 2)
                    link(nc.gpsimd.memset(k_st[KS:KS + 32, :, :, :], 1.0))
                    link(nc.gpsimd.memset(v_t[:].rearrange("p a t h c -> p (a t h c)"), 0.0))
                    nc.gpsimd.memset(v_t[:].rearrange("p a t h c -> p (a t h) c")[:, :, 0:1], 1.0).then_inc(ones_set, 1)
                    pool.wait_ge(ones_set, 1)
                pool.wait_ge(veps_ok, hi)
                nc.gpsimd.tensor_tensor(rstd[:, lo:hi], veps[:, lo:hi], mhalf[:, lo:hi], ALU.pow).then_inc(rstd_ok, hi - lo)

            chain = sem("split_order")
            CH_STEP = 6

            def split(src, parts, n, done):
                apart(pool, 0)
                nc.gpsimd.tensor_scalar(parts[:, 0, :], src, 1.0, 0.0, ALU.mult, ALU.add).then_inc(chain, 1)
                pool.wait_ge(chain, n + 1)
                nc.gpsimd.tensor_tensor(rest[:], src, parts[:, 0, :], ALU.subtract).then_inc(chain, 1)
                pool.wait_ge(chain, n + 2)
                apart(pool, 0)
                nc.gpsimd.tensor_scalar(parts[:, 1, :], rest[:], 1.0, 0.0, ALU.mult, ALU.add).then_inc(chain, 1)
                pool.wait_ge(chain, n + 3)
                nc.gpsimd.tensor_tensor(parts[:, 2, :], rest[:], parts[:, 1, :], ALU.subtract).then_inc(done, 1)

            def split_batch(i, k, off):
                r, s = rs(i, k, off)
                b = RING * r + s
                pool.wait_ge(xn_ok, b + 1)
                r2, s2 = rs(i, k, off - 2)
                pool.wait_ge(scr_out[s2], 96 * (r2 + 1))
                split(xn[:, s % 2, :], q_parts[:, s % 2], CH_STEP * (b - 2), q_split)
                pool.wait_ge(ctx_in[s], 16 * (r + 1))
                pool.wait_ge(q_split, b - 1)
                split(ctx_t[:, s, :], k_parts[:, s % 2], CH_STEP * (b - 2) + 3, k_split)
                pool.wait_ge(k_split, b - 1)

            split_batch(0, 2, 0)
            split_batch(0, 3, 0)

            def step(i, k):
                b = RING * i + k
                if has(i, k, -3):
                    r, s = rs(i, k, -3)
                    pool.wait_ge(u_in[s], 128 * (r + 1))
                    pool.wait_ge(rec_in[s], 128 * (r + 1))
                    if has(i, k, -5):
                        pool.wait_ge(x1_ok, b - 4)
                    nc.gpsimd.tensor_tensor(a_n[:, s % 2, :], u_n[:, s, :], r_n[:, s, :], ALU.mult).then_inc(att_ok, 1)
                if has(i, k, 4):
                    split_batch(i, k, 4)

            def round_weights(m):
                raw = w_raw[m][:].rearrange("p t n -> p (t n)")
                dst = (wg, wu, wd)[m][:].rearrange("p t n -> p (t n)")
                pool.wait_ge(w_exp_ok, m + 1)
                link(nc.gpsimd.tensor_tensor(raw, raw, w_exp[m % 2][:], ALU.add))
                nc.gpsimd.tensor_tensor(dst, raw, w_exp[m % 2][:], ALU.subtract).then_inc(w_ok, 1)

            def step_with_weights(i, k):
                step(i, k)
                if final(i) and k < 3:
                    round_weights(k)

            steps(pool, step_with_weights)

            def rstd_chunk(c):
                pool.wait_ge(v2_ok, CH * (c + 1))
                nc.gpsimd.tensor_tensor(rstd[:, bass.ds(CH * c, CH)], veps[:, bass.ds(CH * c, CH)],
                                        mhalf[:, 0:CH], ALU.pow).then_inc(r2_ok, 1)

            def chunk(c, last):
                for it in range(IT):
                    n = IT * c + it
                    pool.wait_ge(fh_ok, n + 1)
                    nc.gpsimd.tensor_tensor(f_lo[:, it, :], fu[:, it % 2, :], f_hi[:, it, :].bitcast(f32),
                                            ALU.subtract).then_inc(fl_ok, 1)
                    if it == 2 and not last:
                        rstd_chunk(c + 1)

            rstd_chunk(0)
            with pool.Fori(0, NCH - 1) as c:
                chunk(c, False)
            chunk(NCH - 1, True)

        @block.scalar
        def _(act):
            act.wait_ge(gates_in, 48)
            nc.scalar.activation(tanhs[:], gates[:, 0:2], ACT.Tanh).then_inc(tanh_ok, 1)

            def v_out(i, k, off):
                r, s = rs(i, k, off)
                b = RING * r + s
                act.wait_ge(vt_ok, b + 1)
                act.wait_ge(ones_set, 1)
                if has(i, k, off - 2):
                    act.wait_ge(pv_ok, b - 1)
                src = ps[:, PS_M, 0:LT * P].rearrange("p (t h d) -> p t h d", t=LT, h=NH)
                nc.scalar.copy(v_t[:, s % 2, :, :, 1:1 + DH], src).then_inc(vt_sb, 1)

            v_out(0, 0, 0)

            def step(i, k):
                b = RING * i + k
                for p in range(4):
                    if has(i, k, 0):
                        act.wait_ge(st_ok, 4 * b + p + 1)
                        if p == 0 and has(i, k, -2):
                            act.wait_ge(pv_ok, b - 1)
                        bank = PS_ST + 2 * (p % 2)
                        nc.scalar.activation(p_t[:, k % 2, 2 * p:2 * p + 2, :], ps[:, bank:bank + 2, :], ACT.Exp,
                                             scale=DH ** -0.5).then_inc(exp_ok, 1)
                    if p == 1 and has(i, k, -1):
                        r, s = rs(i, k, -1)
                        act.wait_ge(pv_ok, b)
                        if has(i, k, -3):
                            r3, s3 = rs(i, k, -3)
                            act.wait_ge(u_in[s3], 128 * (r3 + 1))
                            act.wait_ge(sum_out[s3], 64 * (r3 + 1))
                        nc.scalar.copy(u_sb[:, s % 2].rearrange("p f l -> p (f l)"), ps[:, PS_U, :]).then_inc(u_ok, 1)
                    if p == 2 and has(i, k, 1):
                        v_out(i, k, 1)

            steps(act, step)

            def chunk_high(c):
                act.wait_ge(t_ok, c + 1)
                nc.scalar.copy(x_t[:, 0], ps[:, PS_T:PS_T + HT, :]).then_inc(hi_ok, 1)

            chunk_high(0)

            def chunk(c, last):
                for it in range(IT):
                    n = IT * c + it
                    act.wait_ge(gu_ok, n + 1)
                    if it >= 2:
                        act.wait_ge(fu_ok, n - 1)
                    nc.scalar.activation(th[:, it % 2, :], ps[:, PS_GU + 2 * (it % 2), :], ACT.Tanh,
                                         scale=gs_half[:, it:it + 1]).then_inc(th_ok, 1)
                    act.wait_ge(fu_ok, n + 1)
                    nc.scalar.copy(f_hi[:, it, :], fu[:, it % 2, :]).then_inc(fh_ok, 1)
                if not last:
                    chunk_high(c + 1)

            act.wait_ge(coef_ok, 1)
            with act.Fori(0, NCH - 1) as c:
                chunk(c, False)
            chunk(NCH - 1, True)

        @block.vector
        def _(v):
            n_dve = [0]

            def link(ins):
                n_dve[0] += 1
                ins.then_inc(dve, 1)
                v.wait_ge(dve, n_dve[0])

            def stats_of(lo, hi):
                for b in range(lo, hi):
                    last = nc.vector.bn_stats(stats[:, b, :], x_sb[:, b, :])
                link(last)
                for b in range(lo, hi):
                    last = nc.vector.bn_aggr(mv[:, b, :], stats[:, b, :])
                link(last)
                nc.vector.tensor_scalar(veps[:, lo:hi], mv[:, lo:hi, 1], EPS, None, ALU.add).then_inc(veps_ok, hi - lo)

            def normalise(b, n):
                v.wait_ge(rstd_ok, b + 1)
                nc.vector.tensor_scalar(xn[:, n, :], x_sb[:, bass.ds(b, 1), :].rearrange("p a l -> p (a l)"),
                                        mv[:, bass.ds(b, 1), 0], rstd[:, bass.ds(b, 1)],
                                        ALU.subtract, ALU.mult).then_inc(xn_ok, 1)

            def split_first(src, parts):
                link(nc.vector.tensor_copy(parts[:, 0, :], src))
                link(nc.vector.tensor_tensor(rest_v[:], src, parts[:, 0, :], ALU.subtract))
                link(nc.vector.tensor_copy(parts[:, 1, :], rest_v[:]))
                link(nc.vector.tensor_tensor(parts[:, 2, :], rest_v[:], parts[:, 1, :], ALU.subtract))

            for b in range(2):
                v.wait_ge(x_in[b], 16)
                stats_of(b, b + 1)
                v.wait_ge(ctx_in[b], 16)
                split_first(ctx_t[:, b, :], k_parts[:, b])
                normalise(b, b)
                v.wait_ge(xn_ok, b + 1)
                split_first(xn[:, b, :], q_parts[:, b])
                v.sem_inc(pre_split, 1)
            for n in range(2, 5):
                lo, hi = pieces[n]
                v.wait_ge(x_in[n], 16)
                stats_of(lo, hi)
                if n == 2:
                    normalise(2, 0)
                    normalise(3, 1)
            v.wait_ge(tanh_ok, 1)
            v.wait_ge(scales_in, 48)
            nc.vector.tensor_tensor(c_att[:], tanhs[:, 0:1], gates[:, 2:3], ALU.mult)
            nc.vector.tensor_scalar(ds_row[:], ds_row[:], tanhs[:, 1:2], None, ALU.mult)
            nc.vector.tensor_scalar(gs_half[:], gs[:], 0.5, None, ALU.mult).then_inc(coef_ok, 1)
            v.wait_ge(coef_ok, 1)
            link(nc.vector.tensor_tensor(gus[:], gs_half[:], us[:], ALU.mult))

            def reduce_max(n, before, h, quad):
                v.wait_ge(s_ok, n + 1)
                if h == 0 and before is not None:
                    v.wait_ge(mt_ok, before)
                nc.vector.tensor_reduce(neg_max[:, quad, LT * h:LT * (h + 1)],
                                        ps[:, PS_S + h % 2, :].rearrange("p (t l) -> p t l", t=LT),
                                        axis=AX.X, op=ALU.max, negate=True).then_inc(max_ok, 1)

            def split_max(i, k, off, quad):
                r, s = rs(i, k, off)
                b = RING * r + s
                v.wait_ge(mt_ok, 2 * b + quad + 1)
                if has(i, k, off - 1):
                    r1, s1 = rs(i, k, off - 1)
                    v.wait_ge(mx_in[quad][s1], 32 * (r1 + 1))
                src = ps[0:QUAD * LT, PS_M, 0:P]
                nc.vector.tensor_copy(max_t[:, quad, 0, :], src).then_inc(mt_hi, 1)
                v.wait_ge(mt_hi, 2 * b + quad + 1)
                nc.vector.tensor_tensor(max_t[:, quad, 1, :], src, max_t[:, quad, 0, :],
                                        ALU.subtract).then_inc(mt_split, 1)

            for idx in range(8):
                reduce_max(idx, None, idx % 4, idx // 4)
                if idx == 5:
                    split_max(0, 0, 0, 0)
            for idx in range(8, 12):
                reduce_max(idx, 1, idx % 4, 0)
                if idx == 9:
                    split_max(0, 0, 0, 1)

            def step(i, k):
                b = RING * i + k
                if has(i, k, 4):
                    v.wait_ge(q_split, b + 1)
                    normalise(b + 4, k % 2)
                for n in range(8):
                    if has(i, k, 1 if n < 4 else 2):
                        reduce_max(8 * b + 12 + n, 2 * b + 2 + n // 4, n % 4, 1 if n < 4 else 0)
                    if n == 1 and has(i, k, 1):
                        split_max(i, k, 1, 0)
                    if n == 2 and has(i, k, -2):
                        r, s = rs(i, k, -2)
                        v.wait_ge(sum_in[s], 16 * (r + 1))
                        nc.vector.reciprocal(r_sp[:, s, :], s_sp[:, s, :]).then_inc(rec_ok, 1)
                    if n == 3 and has(i, k, -3):
                        r, s = rs(i, k, -3)
                        v.wait_ge(att_ok, b - 2)
                        xb = x_sb[:, bass.ds(b - 3, 1), :].rearrange("p a l -> p (a l)")
                        nc.vector.scalar_tensor_tensor(xb, a_n[:, s % 2, :], c_att[:, 0:1], xb,
                                                       ALU.mult, ALU.add).then_inc(x1_ok, 1)
                    if n == 5 and has(i, k, 1):
                        split_max(i, k, 1, 1)

            def binades(m):
                raw = w_raw[m][:].rearrange("p t n -> p (t n)")
                if m == 2:
                    v.wait_ge(w_ok, 1)
                link(nc.vector.tensor_scalar(w_exp[m % 2][:].bitcast(u32), raw.bitcast(u32), 0x7F800000, None,
                                             ALU.bitwise_and))
                nc.vector.tensor_scalar(w_exp[m % 2][:], w_exp[m % 2][:], E4M3_MIN_EXP, E4M3_MAGIC,
                                        ALU.max, ALU.mult).then_inc(w_exp_ok, 1)

            def norm_chunk(c):
                for q in range(CH):
                    t = CH * c + q
                    v.wait_ge(x1_ok, t + 1)
                    nc.vector.bn_stats(stats[:, q, :], x_sb[:, bass.ds(t, 1), :].rearrange("p a l -> p (a l)")
                                       ).then_inc(n2_stats, 1)
                for q in range(CH):
                    v.wait_ge(n2_stats, CH * c + q + 1)
                    apart(v, 1)
                    nc.vector.bn_aggr(mv[:, q, :], stats[:, q, :]).then_inc(n2_aggr, 1)
                v.wait_ge(n2_aggr, CH * c + CH)
                nc.vector.tensor_scalar(veps[:, bass.ds(CH * c, CH)], mv[:, 0:CH, 1], EPS, None,
                                        ALU.add).then_inc(v2_ok, CH)

            def norm_apply(c):
                v.wait_ge(r2_ok, c + 1)
                if not isinstance(c, int) or c > 0:
                    v.wait_ge(t_ok, c)
                for q in range(CH):
                    t = CH * c + q
                    nc.vector.tensor_scalar(xn2[:, q, :], x_sb[:, bass.ds(t, 1), :].rearrange("p a l -> p (a l)"),
                                            mv[:, q, 0:1], rstd[:, bass.ds(t, 1)],
                                            ALU.subtract, ALU.mult).then_inc(n2_ok, 1)

            def chunk_low(c):
                v.wait_ge(hi_ok, c + 1)
                nc.vector.tensor_tensor(x_t[:, 1], ps[:, PS_T:PS_T + HT, :], x_t[:, 0],
                                        ALU.subtract).then_inc(lo_ok, 1)

            def step_v(i, k):
                if final(i) and k == 0:
                    v.wait_ge(w_in, 48)
                    binades(0)
                    binades(1)
                if final(i) and k == 2:
                    binades(2)
                step(i, k)

            steps(v, step_v)
            norm_chunk(0)
            norm_apply(0)
            chunk_low(0)

            def chunk(c, last):
                for it in range(IT):
                    n = IT * c + it
                    v.wait_ge(th_ok, n + 1)
                    nc.vector.scalar_tensor_tensor(ga[:, it % 2, :], th[:, it % 2, :], 1.0,
                                                   ps[:, PS_GU + 2 * (it % 2), :], ALU.add, ALU.mult).then_inc(ga_ok, 1)
                    v.wait_ge(ga_ok, n + 1)
                    if it >= 2 or not isinstance(c, int) or c > 0:
                        v.wait_ge(fl_ok, n - 1)
                    nc.vector.scalar_tensor_tensor(fu[:, it % 2, :], ps[:, PS_GU + 2 * (it % 2) + 1, :],
                                                   gus[:, it:it + 1], ga[:, it % 2, :],
                                                   ALU.mult, ALU.mult).then_inc(fu_ok, 1)
                    if it == 1 and not last:
                        norm_chunk(c + 1)
                    if it == 3 and not last:
                        norm_apply(c + 1)
                if not last:
                    chunk_low(c + 1)
                for q in range(CH):
                    t = CH * c + q
                    n = q % 2
                    v.wait_ge(y_ok, t + 1)
                    nc.vector.tensor_tensor(yo[:, n, :], ps[:, PS_Y + n, 0:L], ds_row[:], ALU.mult).then_inc(yo_ok, 1)
                    v.wait_ge(yo_ok, t + 1)
                    if q >= 2 or not isinstance(c, int) or c > 0:
                        v.wait_ge(out_ok[n], 16 * (2 * c + q // 2))
                    nc.vector.tensor_tensor(o_sb[:, n, :], yo[:, n, :],
                                            x_sb[:, bass.ds(t, 1), :].rearrange("p a l -> p (a l)"),
                                            ALU.add).then_inc(o_ok, 1)

            chunk(0, False)
            with v.Fori(1, NCH - 1) as c:
                chunk(c, False)
            chunk(NCH - 1, True)

        @block.tensor
        def _(pe):
            def scores(idx, r, s, h):
                if not isinstance(idx, int) or idx >= 2:
                    pe.wait_ge(max_ok, idx - 1)
                for t in range(LT):
                    last = nc.tensor.matmul(ps[:, PS_S + h % 2, L * t:L * (t + 1)],
                                            q_st[0:KS, s, h, P * t:P * (t + 1)], k_st[0:KS, s, h, :],
                                            start=True, stop=True)
                last.then_inc(s_ok, 1)

            def scores_t(i, k, p):
                b = RING * i + k
                if p % 2 == 0:
                    pe.wait_ge(mx_in[p // 2][k], 32 * (i + 1))
                if p >= 2 or has(i, k, -1):
                    pe.wait_ge(exp_ok, 4 * b + p - 1)
                for m in range(2):
                    h = 2 * p + m
                    for t in range(LT):
                        last = nc.tensor.matmul(ps[:, PS_ST + 2 * (p % 2) + m, L * t:L * (t + 1)],
                                                k_st[0:KS + MAXROWS, k, h, P * t:P * (t + 1)],
                                                q_st[0:KS + MAXROWS, k, h, :], start=True, stop=True)
                last.then_inc(st_ok, 1)

            def transpose_max(i, k, off, quad):
                r, s = rs(i, k, off)
                b = RING * r + s
                pe.wait_ge(max_ok, 8 * b + 4 * (quad + 1))
                if quad == 0:
                    if has(i, k, off - 1):
                        pe.wait_ge(mt_split, 2 * b)
                    pe.wait_ge(vt_sb, b if has(i, k, off - 1) else 1)
                else:
                    pe.wait_ge(mt_split, 2 * b + 1)
                    pe.wait_ge(vt_sb, b + 1)
                nc.tensor.transpose(ps[0:QUAD * LT, PS_M, 0:P], neg_max[:, quad, :], ident[:]).then_inc(mt_ok, 1)

            def transpose_ctx(i, k, off):
                r, s = rs(i, k, off)
                b = RING * r + s
                pe.wait_ge(ctx_in[s], 16 * (r + 1))
                if has(i, k, off - 1):
                    pe.wait_ge(mt_split, 2 * b + 1)
                for t in range(LT):
                    last = nc.tensor.transpose(ps[:, PS_M, P * t:P * (t + 1)], ctx_t[:, s, P * t:P * (t + 1)], ident[:])
                last.then_inc(vt_ok, 1)

            def weighted(i, k, off, quad):
                r, s = rs(i, k, off)
                b = RING * r + s
                pe.wait_ge(exp_ok, 4 * b + 2 * (quad + 1))
                if quad == 0:
                    pe.wait_ge(vt_sb, b + 1)
                    if has(i, k, off - 1):
                        pe.wait_ge(u_ok, b)
                for t in range(LT):
                    for j in range(QUAD):
                        h = QUAD * quad + j
                        last = nc.tensor.matmul(ps[32 * j:32 * (j + 1), PS_U, L * quad:L * (quad + 1)],
                                                v_t[:, s % 2, t, h, :], p_t[:, s % 2, h, L * t:L * (t + 1)],
                                                start=(t == 0), stop=(t == LT - 1))
                if quad == 1:
                    last.then_inc(pv_ok, 1)

            pe.wait_ge(consts, 2)
            transpose_ctx(0, 0, 0)
            pe.wait_ge(st_in[0], 144)
            for idx in range(8):
                scores(idx, 0, 0, idx)
                if idx == 5:
                    transpose_max(0, 0, 0, 0)
            pe.wait_ge(st_in[1], 144)
            for idx in range(8, 12):
                scores(idx, 0, 1, idx - 8)
                if idx == 9:
                    transpose_max(0, 0, 0, 1)
            pe.wait_ge(ones_set, 1)

            def step(i, k):
                b = RING * i + k
                for p in range(4):
                    if has(i, k, 0):
                        scores_t(i, k, p)
                    off = 1 if p < 2 else 2
                    if has(i, k, off):
                        r, s = rs(i, k, off)
                        if p == 2:
                            pe.wait_ge(st_in[s], 144 * (r + 1))
                        for m in range(2):
                            n = 2 * p + m
                            scores(8 * b + 12 + n, r, s, (n + 4) % 8)
                    if p == 0 and has(i, k, 1):
                        transpose_max(i, k, 1, 0)
                    if p == 0 and has(i, k, -1):
                        weighted(i, k, -1, 1)
                    if p == 1 and has(i, k, 1):
                        transpose_ctx(i, k, 1)
                    if p == 2 and has(i, k, 1):
                        transpose_max(i, k, 1, 1)
                    if p == 2 and has(i, k, 0):
                        weighted(i, k, 0, 0)

            steps(pe, step)

            def transposes(c):
                pe.wait_ge(n2_ok, CH * (c + 1))
                for q in range(CH):
                    for ht in range(HT):
                        last = nc.tensor.transpose(ps[:, PS_T + ht, P * q:P * (q + 1)],
                                                   xn2[:, q, P * ht:P * (ht + 1)], ident[:])
                last.then_inc(t_ok, 1)

            def gate_up(c):
                pe.wait_ge(lo_ok, c + 1)
                for it in range(IT):
                    n = IT * c + it
                    if it >= 2 or not isinstance(c, int) or c > 0:
                        pe.wait_ge(fu_ok, n - 1)
                    for m, w in enumerate((wg, wu)):
                        for j in range(2 * HT):
                            ht, part = j // 2, j % 2
                            last = nc.tensor.matmul(ps[:, PS_GU + 2 * (it % 2) + m, :], w[:, ht, P * it:P * (it + 1)],
                                                    x_t[:, part, ht, :], start=(j == 0), stop=(j == 2 * HT - 1))
                    last.then_inc(gu_ok, 1)

            def down(c):
                pe.wait_ge(fl_ok, IT * (c + 1))
                for q in range(CH):
                    t = CH * c + q
                    if q >= 2 or not isinstance(c, int) or c > 0:
                        pe.wait_ge(yo_ok, t - 1)
                    for j in range(2 * IT):
                        it, f = j // 2, (f_hi, f_lo)[j % 2]
                        last = nc.tensor.matmul(ps[:, PS_Y + q % 2, 0:L], f[:, it, P * q:P * (q + 1)],
                                                wd[:, it, :], start=(j == 0), stop=(j == 2 * IT - 1))
                    last.then_inc(y_ok, 1)

            pe.wait_ge(u_ok, NB)
            pe.wait_ge(mt_split, 2 * NB)
            transposes(0)
            pe.wait_ge(w_ok, 3)

            def chunk(c, last):
                gate_up(c)
                if not last:
                    transposes(c + 1)
                down(c)

            chunk(0, False)
            with pe.Fori(1, NCH - 1) as c:
                chunk(c, False)
            chunk(NCH - 1, True)


_INS = ["x", "ctx_2048", "g_xattn", "g_ffn", "L0_xattn_gamma", "L0_ffn_gate_w", "L0_ffn_up_w", "L0_ffn_down_w",
        "L0_ffn_gate_scale", "L0_ffn_up_scale", "L0_ffn_down_scale"]


def kernel(**inputs):
    import numpy as np
    import concourse.bacc as bacc
    from concourse import mybir
    from concourse.bass_utils import run_bass_kernel_spmd

    nc = bacc.Bacc("TRN2", target_bir_lowering=False, num_devices=1)
    arrays, args = {}, []
    for name in _INS:
        a = np.ascontiguousarray(inputs[name])
        if a.ndim == 0:
            a = a.reshape(1)
        arrays[f"in_{name}"] = a
        args.append(nc.dram_tensor(f"in_{name}", a.shape, mybir.dt.from_np(a.dtype), kind="ExternalInput").ap())
    shape = (NB, D, L)
    result = nc.dram_tensor("out_x", shape, mybir.dt.float32, kind="ExternalOutput").ap()
    build(nc, *args, result)
    r = run_bass_kernel_spmd(nc, [arrays], core_ids=[0])
    return r.results[0]["out_x"]
```

```python
import concourse.bass as bass
from concourse import mybir
from contextlib import ExitStack

NB = 16
D = 128
L = 256
NH = 8
DH = D // NH
P = 128
LT = L // P
NPART = 3
GB = P // DH
NG = NB // GB
HH = NH // 2
NPROD = 6
Q_RUNS = [(0, 3, 0, 0), (3, 2, 1, 0), (5, 1, 2, 0)]
K_RUNS = [(0, 3, 0, 1), (3, 2, 0, 1), (5, 1, 0, 1)]
KS = DH * NPROD
MAXROWS = 2
RING = 4
QUAD = 4
SLOTW = 32
I = 768
IT = I // P
HT = L // P
CH = 4
NCH = NB // CH
TOK = CH * P
EPS = 1e-5
E4M3_MIN_EXP = 2.0 ** -6
E4M3_MAGIC = 1.5 * 2.0 ** 20


def build(nc, x, ctx, g_xattn, g_ffn, gamma, gate_w, up_w, down_w, gate_scale, up_scale, down_scale, out):
    f32, f32r, bf16, f16, u32 = (mybir.dt.float32, mybir.dt.float32r, mybir.dt.bfloat16,
                                 mybir.dt.float16, mybir.dt.uint32)
    ALU = mybir.AluOpType
    ACT = mybir.ActivationFunctionType
    AX = mybir.AxisListType

    es = ExitStack()
    with es:
        def sb(name, shape, dt=f32):
            return es.enter_context(nc.sbuf_tensor(name, shape, dt))

        def sem(name):
            return es.enter_context(nc.semaphore(name))

        def sems(name, n=RING):
            return [sem(f"{name}{j}") for j in range(n)]

        stacks = nc.dram_tensor("stacks", (NB, DH, NPROD, 2, NH, L), bf16, kind="Internal").ap()
        u_scr = nc.dram_tensor("u_scr", (NB, QUAD, P // QUAD, 2, L), f32, kind="Internal").ap()
        r_scr = nc.dram_tensor("r_scr", (NB, 2, QUAD, L), f32, kind="Internal").ap()

        ident = sb("ident", [P, P])
        x_sb = sb("x_sb", [P, NG * NH, L])
        c_sb = sb("c_sb", [P, NG * NH, L])
        xn = sb("xn", [P, NH, L])
        rest = sb("rest", [P, HH, L])
        q_parts = sb("q_parts", [P, NPART, NH, L], bf16)
        k_parts = sb("k_parts", [P, NPART, NH, L], bf16)
        ctx_t = sb("ctx_t", [P, RING, L])
        st = sb("st", [P, RING, 2, NH, L], bf16)
        q_st, k_st = st[:, :, 0], st[:, :, 1]
        neg_max = sb("neg_max", [P, 2, QUAD * LT])
        max_t = sb("max_t", [QUAD * LT, 2, MAXROWS, P], bf16)
        p_t = sb("p_t", [P, 2, NH, LT * L])
        rest_v = p_t[:, 1, 0:2, :].rearrange("p a l -> p (a l)").rearrange("p (h l) -> p h l", h=HH)
        v_t = sb("v_t", [P, 2, LT, NH, SLOTW])
        u_sb = sb("u_sb", [P, 2, 2, L])
        s_sp = sb("s_sp", [P, GB * NH * L // P])
        r_sp = sb("r_sp", [P, GB * NH * L // P])
        u_n, r_n = c_sb[:, 0:NH, :], c_sb[:, NH:2 * NH, :]
        stats = sb("stats", [P, NB, 6])
        mv = sb("mv", [P, NB, 2])
        veps = sb("veps", [P, NB])
        rstd = sb("rstd", [P, NB])
        mhalf = sb("mhalf", [P, NB])
        gates = sb("gates", [P, 3])
        tanhs = sb("tanhs", [P, 2])
        c_att = sb("c_att", [P, 1])
        gs = sb("gs", [P, IT])
        us = sb("us", [P, IT])
        gs_half = sb("gs_half", [P, IT])
        gus = sb("gus", [P, IT])
        ds_row = sb("ds_row", [P, L])
        w_raw = [sb("wg_raw", [P, HT, I]), sb("wu_raw", [P, HT, I]), sb("wd_raw", [P, IT, L])]
        w_exp = k_parts[:].rearrange("p c h l -> p (c h l)")[:, 0:2 * HT * I].bitcast(f32)
        wg = sb("wg", [P, HT, I], f16)
        wu = sb("wu", [P, HT, I], f16)
        wd = sb("wd", [P, IT, L], f32r)
        xn2 = xn[:, 0:CH, :]
        x_t = q_parts[:].rearrange("p c h l -> p (c h l)")[:, 0:2 * HT * TOK].bitcast(f16).rearrange(
            "p (a t n) -> p a t n", a=2, t=HT)
        th, ga, fu = (p_t[:, 0, 2 * m:2 * m + 2, :] for m in range(3))
        f_hi = sb("f_hi", [P, IT, TOK], f32r)
        f_lo = sb("f_lo", [P, IT, TOK], f32r)
        yo = sb("yo", [P, 2, L])
        o_sb = sb("o_sb", [P, 2, L])
        ps = es.enter_context(nc.psum_tensor("ps", [P, 8, 512], f32))
        PS_S, PS_ST, PS_U, PS_M = 0, 2, 6, 7
        PS_GU, PS_T, PS_Y = 0, 4, 6

        x_in = sems("x_in", 2 * NG)
        c_in = sems("c_in", 2 * NG)
        ctx_in = sems("ctx_in")
        gates_in = sem("gates_in")
        scales_in = sem("scales_in")
        w_in = sem("w_in")
        consts = sem("consts")
        ones_set = sem("ones_set")
        veps_ok = sem("veps_ok")
        rstd_ok = sem("rstd_ok")
        tanh_ok = sem("tanh_ok")
        coef_ok = sem("coef_ok")
        xn_ok = sem("xn_ok")
        q_split0 = sem("q_split0")
        q_split1 = sem("q_split1")
        k_hi = sem("k_hi")
        k_rest = sem("k_rest")
        k_split0 = sem("k_split0")
        k_split1 = sem("k_split1")
        scr_out = sems("scr_out", 2 * NG)
        st_in = sems("st_in")
        mx_in = [sems(f"mx_in{q}_") for q in range(2)]
        s_ok = sem("s_ok")
        max_ok = sem("max_ok")
        mt_ok = sem("mt_ok")
        mt_hi = sem("mt_hi")
        mt_split = sem("mt_split")
        st_ok = sem("st_ok")
        exp_ok = sem("exp_ok")
        vt_ok = sem("vt_ok")
        vt_sb = sem("vt_sb")
        pv_ok = sem("pv_ok")
        u_ok = sem("u_ok")
        u_out = sems("u_out")
        u_in = sems("u_in", NG)
        sum_in = sems("sum_in", NG)
        rec_ok = sem("rec_ok")
        rec_out = sems("rec_out", NG)
        rec_in = sems("rec_in", NG)
        att_ok = sem("att_ok")
        x1_ok = sem("x1_ok")
        dve = sem("dve_order")
        pool_o = sem("pool_order")
        taken = sems("taken", 2)
        w_exp_ok = sem("w_exp_ok")
        w_ok = sem("w_ok")
        v2_ok = sem("v2_ok")
        r2_ok = sem("r2_ok")
        n2_ok = sem("n2_ok")
        t_ok = sem("t_ok")
        hi_ok = sem("hi_ok")
        lo_ok = sem("lo_ok")
        gu_ok = sem("gu_ok")
        th_ok = sem("th_ok")
        fu_ok = sem("fu_ok")
        fh_ok = sem("fh_ok")
        fl_ok = sem("fl_ok")
        y_ok = sem("y_ok")
        o_ok = sem("o_ok")
        out_ok = sems("out_ok", 2)
        n2_stats = sem("n2_stats")
        n2_aggr = sem("n2_aggr")
        ga_ok = sem("ga_ok")
        yo_ok = sem("yo_ok")

        block = es.enter_context(nc.Block())

        def has(i, k, off):
            return not isinstance(i, int) or 0 <= RING * i + k + off < NB

        def apart(eng, which):
            eng.sem_inc(taken[which], 1)

        def first(i):
            return isinstance(i, int) and i == 0

        def final(i):
            return isinstance(i, int) and i == NB // RING - 1

        def rs(i, k, off):
            return i + (k + off) // RING, (k + off) % RING

        def steps(eng, step):
            for k in range(RING):
                step(0, k)
            with eng.Fori(1, NB // RING - 1) as i:
                for k in range(RING):
                    step(i, k)
            for k in range(RING):
                step(NB // RING - 1, k)
            step(NB // RING, 0)

        @block.sync
        def _(sp):
            def load_ctx(b, slot):
                sp.dma_start(ctx_t[:, slot, :], ctx[bass.ds(b, 1)].rearrange("a p l -> (a p) l")
                             ).then_inc(ctx_in[slot], 16)

            def load_half(src, dst, done, n):
                g = n // 2
                for h in range(HH * (n % 2), HH * (n % 2 + 1)):
                    sp.dma_start(dst[:, NH * g + h, :], src[GB * g:GB * (g + 1), DH * h:DH * (h + 1), :]
                                 ).then_inc(done[n], 16)

            def save_half(n, parts, m, runs):
                g, h = n // 2, HH * (n % 2)
                dst = stacks[GB * g:GB * (g + 1), :, :, m, h:h + HH, :].rearrange("b d c h l -> (b d) c (h l)")
                for c, count, part, step in runs:
                    src = parts[:, part:part + (count if step else 1), h:h + HH, :].rearrange("p c h l -> p c (h l)")
                    if not step:
                        src = src.broadcast_to([P, count, HH * L])
                    sp.dma_start(dst[:, c:c + count, :], src).then_inc(scr_out[n], 16)

            def load_stacks(b, i, s):
                if isinstance(b, int):
                    sp.wait_ge(scr_out[2 * (b // GB)], 96)
                    sp.wait_ge(scr_out[2 * (b // GB) + 1], 96)
                sp.dma_start(st[0:KS, s], stacks[bass.ds(b, 1)].rearrange("a d c m h l -> (a d c) m h l")
                             ).then_inc(st_in[s], 16)

            def load_maxima(i, k, off, quad):
                r, s = rs(i, k, off)
                sp.wait_ge(mt_split, 2 * (RING * r + s) + quad + 1)
                for part in range(MAXROWS):
                    dst = q_st[KS + part:KS + part + 1, s, QUAD * quad:QUAD * (quad + 1)]
                    sp.dma_start(dst.rearrange("p h l -> p (h l)"),
                                 max_t[:, quad, part, :]).then_inc(mx_in[quad][s], 16)

            load_half(ctx, c_sb, c_in, 0)
            load_half(x, x_sb, x_in, 0)
            load_half(ctx, c_sb, c_in, 1)
            load_half(x, x_sb, x_in, 1)
            for dst, src in ((gates[:, 0:1], g_xattn), (gates[:, 1:2], g_ffn), (gates[:, 2:3], gamma)):
                sp.dma_start(dst, src.rearrange("(a c) -> a c", c=1).broadcast_to([P, 1])).then_inc(gates_in, 16)
            load_ctx(0, 0)
            for n in range(2):
                sp.wait_ge(q_split0, n + 1)
                save_half(n, q_parts, 0, Q_RUNS)
                sp.wait_ge(k_split0, n + 1)
                save_half(n, k_parts, 1, K_RUNS)
            for b in range(3):
                load_stacks(b, 0, b)
                load_ctx(b + 1, b + 1)
            load_half(ctx, c_sb, c_in, 2)
            load_half(ctx, c_sb, c_in, 3)
            load_half(x, x_sb, x_in, 2)
            load_half(x, x_sb, x_in, 3)
            load_maxima(0, 0, 0, 0)
            load_maxima(0, 0, 0, 1)

            def save_second(n):
                sp.wait_ge(k_split1, n - 1)
                save_half(n, k_parts, 1, K_RUNS)
                sp.wait_ge(q_split1, n - 1)
                save_half(n, q_parts, 0, Q_RUNS)

            def load_sums(g):
                for b in range(GB * g, GB * (g + 1)):
                    sp.wait_ge(u_out[b % RING], 16 * (b // RING + 1))
                if g:
                    sp.wait_ge(x1_ok, 2)
                else:
                    sp.wait_ge(k_split0, 2)
                    sp.wait_ge(k_split1, 2)
                u = u_scr[GB * g:GB * (g + 1)]
                for half in range(2):
                    sp.dma_start(s_sp[64 * half:64 * (half + 1), :], u[:, :, 0, half, :]).then_inc(sum_in[g], 16)
                for half in range(2):
                    for j in range(QUAD):
                        sp.dma_start(u_n[:, QUAD * half + j, :], u[:, j, 1:1 + DH, half, :]).then_inc(u_in[g], 16)

            def load_reciprocals(g):
                sp.wait_ge(rec_ok, g + 1)
                r = r_scr[GB * g:GB * (g + 1)]
                for half in range(2):
                    sp.dma_start(r[:, half].rearrange("b j l -> b (j l)"), r_sp[64 * half:64 * (half + 1), :]
                                 ).then_inc(rec_out[g], 16)
                sp.wait_ge(rec_out[g], 32)
                src = r.rearrange("b f j l -> b (f j l)")
                src = src.rearrange("b (a n) -> b a n", a=1).broadcast_to([GB, DH, NH * L])
                sp.dma_start(r_n.rearrange("p h l -> p (h l)"), src).then_inc(rec_in[g], 16)

            def step(i, k):
                b = RING * i + k
                if has(i, k, 1):
                    load_maxima(i, k, 1, 0)
                if has(i, k, -1):
                    r, s = rs(i, k, -1)
                    sp.wait_ge(u_ok, b)
                    sp.dma_start(u_scr[bass.ds(b - 1, 1)].rearrange("a j r f l -> (a j r) (f l)"),
                                 u_sb[:, s % 2].rearrange("p f l -> p (f l)")).then_inc(u_out[s], 16)
                if has(i, k, 4):
                    sp.wait_ge(vt_ok, b + 1)
                    load_ctx(b + 4, k)
                if has(i, k, 3):
                    if has(i, k, -1):
                        sp.wait_ge(st_ok, 4 * b)
                    load_stacks(b + 3, i, (k + 3) % RING)
                if has(i, k, 1):
                    load_maxima(i, k, 1, 1)
                if first(i):
                    if k == 0:
                        for dst, src in ((w_raw[0], gate_w), (w_raw[1], up_w), (w_raw[2], down_w)):
                            sp.dma_start(dst[:], src.rearrange("(t p) n -> p t n", p=P)).then_inc(w_in, 16)
                        sp.dma_start(gs[:], gate_scale.rearrange("(t p) -> p t", p=P),
                                     allow_slow_non_contiguous=True).then_inc(scales_in, 16)
                        sp.dma_start(us[:], up_scale.rearrange("(t p) -> p t", p=P),
                                     allow_slow_non_contiguous=True).then_inc(scales_in, 16)
                        sp.dma_start(ds_row[:], down_scale.rearrange("(a c) -> a c", a=1).broadcast_to([P, L])
                                     ).then_inc(scales_in, 16)
                    if k == SAVE_AT[0]:
                        save_second(2)
                    if k == SAVE_AT[1]:
                        save_second(3)
                        sp.wait_ge(scr_out[2], 96)
                        sp.wait_ge(scr_out[3], 96)
                if final(i) and k == 0:
                    load_sums(0)
                if final(i) and k == 1:
                    load_reciprocals(0)

            SAVE_AT = (2, 3)
            steps(sp, step)

            load_sums(1)
            load_reciprocals(1)

            def store(g, h, n, done):
                sp.wait_ge(o_ok, done + 1)
                sp.dma_start(out[GB * g:GB * (g + 1), bass.ds(DH * h, DH), :], o_sb[:, n, :]).then_inc(out_ok[n], 16)

            for g in range(NG):
                with sp.Fori(0, NH // 2) as j:
                    for n in range(2):
                        store(g, 2 * j + n, n, NH * g + 2 * j + n)
            for n in range(2):
                sp.wait_ge(out_ok[n], 16 * (NB // 2))

        @block.gpsimd
        def _(pool):
            n_pool = [0]

            def link(ins):
                n_pool[0] += 1
                ins.then_inc(pool_o, 1)
                pool.wait_ge(pool_o, n_pool[0])

            link(nc.gpsimd.memset(ident[:], 0.0))
            nc.gpsimd.affine_select(out=ident[:], in_=ident[:], compare_op=ALU.not_equal, fill=1.0, base=0,
                                    pattern=[[-1, P]], channel_multiplier=1).then_inc(consts, 1)
            nc.gpsimd.memset(mhalf[:], -0.5).then_inc(consts, 1)
            pool.wait_ge(consts, 2)
            def rstd_half(n):
                pool.wait_ge(veps_ok, n + 1)
                at = slice(HH * n, HH * (n + 1))
                nc.gpsimd.tensor_tensor(rstd[:, at], veps[:, at], mhalf[:, at], ALU.pow).then_inc(rstd_ok, 1)

            def heads(n):
                return slice(HH * (n % 2), HH * (n % 2 + 1))

            def flat(ap):
                return ap.rearrange("p h l -> p (h l)")

            for n in range(2):
                k, part = flat(c_sb[:, HH * n:HH * (n + 1), :]), k_parts[:, :, heads(n), :]
                pool.wait_ge(c_in[n], 16 * HH)
                pool.wait_ge(k_hi, 2 * n + 1)
                if n:
                    pool.wait_ge(k_split0, n)
                nc.gpsimd.tensor_tensor(flat(rest[:]), k, flat(part[:, 0]), ALU.subtract).then_inc(k_rest, 1)
                rstd_half(n)
                pool.wait_ge(k_hi, 2 * n + 2)
                nc.gpsimd.tensor_tensor(flat(part[:, 2]), flat(rest[:]), flat(part[:, 1]), ALU.subtract).then_inc(k_split0, 1)
            pool.wait_ge(rstd_ok, 2)
            pool.wait_ge(k_split0, 2)
            for s in range(RING):
                link(nc.gpsimd.memset(flat(k_st[KS:KS + 32, s]), 1.0))
            link(nc.gpsimd.memset(v_t[:].rearrange("p a t h c -> p (a t h c)"), 0.0))
            nc.gpsimd.memset(v_t[:].rearrange("p a t h c -> p (a t h) c")[:, :, 0:1], 1.0).then_inc(ones_set, 1)
            pool.wait_ge(ones_set, 1)

            def split(src, part, done, count):
                link(nc.gpsimd.tensor_scalar(flat(part[:, 0]), src, 1.0, 0.0, ALU.mult, ALU.add))
                link(nc.gpsimd.tensor_tensor(flat(rest[:]), src, flat(part[:, 0]), ALU.subtract))
                link(nc.gpsimd.tensor_scalar(flat(part[:, 1]), flat(rest[:]), 1.0, 0.0, ALU.mult, ALU.add))
                nc.gpsimd.tensor_tensor(flat(part[:, 2]), flat(rest[:]), flat(part[:, 1]),
                                        ALU.subtract).then_inc(done, 1)
                pool.wait_ge(done, count)

            for n in (2, 3):
                pool.wait_ge(c_in[n], 16 * HH)
                pool.wait_ge(scr_out[n - 2], 96)
                split(flat(c_sb[:, HH * n:HH * (n + 1), :]), k_parts[:, :, heads(n), :], k_split1, n - 1)
                rstd_half(n)
                pool.wait_ge(xn_ok, HH * (n + 1))
                split(flat(xn[:, heads(n), :]), q_parts[:, :, heads(n), :], q_split1, n - 1)

            for m, w in enumerate((wg, wu, wd)):
                raw = w_raw[m][:].rearrange("p t n -> p (t n)")
                pool.wait_ge(w_exp_ok, m + 1)
                link(nc.gpsimd.tensor_tensor(raw, raw, w_exp, ALU.add))
                nc.gpsimd.tensor_tensor(w[:].rearrange("p t n -> p (t n)"), raw, w_exp,
                                        ALU.subtract).then_inc(w_ok, 1)

            def attention(g):
                pool.wait_ge(u_in[g], 128)
                pool.wait_ge(rec_in[g], 16)
                for n in range(2):
                    u = flat(u_n[:, heads(n), :])
                    nc.gpsimd.tensor_tensor(u, u, flat(r_n[:, heads(n), :]), ALU.mult).then_inc(att_ok, 1)

            attention(0)

            def rstd_chunk(c):
                pool.wait_ge(v2_ok, CH * (c + 1))
                nc.gpsimd.tensor_tensor(rstd[:, bass.ds(CH * c, CH)], veps[:, bass.ds(CH * c, CH)],
                                        mhalf[:, 0:CH], ALU.pow).then_inc(r2_ok, 1)

            def chunk(c, last):
                for it in range(IT):
                    n = IT * c + it
                    pool.wait_ge(fh_ok, n + 1)
                    nc.gpsimd.tensor_tensor(f_lo[:, it, :], fu[:, it % 2, :], f_hi[:, it, :].bitcast(f32),
                                            ALU.subtract).then_inc(fl_ok, 1)
                    if it == 2 and not last:
                        rstd_chunk(c + 1)

            rstd_chunk(0)
            attention(1)
            with pool.Fori(0, NCH - 1) as c:
                chunk(c, False)
            chunk(NCH - 1, True)

        @block.scalar
        def _(act):
            for n in range(2):
                at = slice(HH * n, HH * (n + 1))
                act.wait_ge(c_in[n], 16 * HH)
                nc.scalar.copy(k_parts[:, 0, at, :], c_sb[:, at, :]).then_inc(k_hi, 1)
                act.wait_ge(k_rest, n + 1)
                nc.scalar.copy(k_parts[:, 1, at, :], rest[:]).then_inc(k_hi, 1)
            act.wait_ge(gates_in, 48)
            nc.scalar.activation(tanhs[:], gates[:, 0:2], ACT.Tanh).then_inc(tanh_ok, 1)

            def v_out(i, k, off):
                r, s = rs(i, k, off)
                b = RING * r + s
                act.wait_ge(vt_ok, b + 1)
                act.wait_ge(ones_set, 1)
                if has(i, k, off - 2):
                    act.wait_ge(pv_ok, b - 1)
                src = ps[:, PS_M, 0:LT * P].rearrange("p (t h d) -> p t h d", t=LT, h=NH)
                nc.scalar.copy(v_t[:, s % 2, :, :, 1:1 + DH], src).then_inc(vt_sb, 1)

            v_out(0, 0, 0)

            def step(i, k):
                b = RING * i + k
                for p in range(4):
                    if has(i, k, 0):
                        act.wait_ge(st_ok, 4 * b + p + 1)
                        if p == 0 and has(i, k, -2):
                            act.wait_ge(pv_ok, b - 1)
                        bank = PS_ST + 2 * (p % 2)
                        nc.scalar.activation(p_t[:, k % 2, 2 * p:2 * p + 2, :], ps[:, bank:bank + 2, :], ACT.Exp,
                                             scale=DH ** -0.5).then_inc(exp_ok, 1)
                    if p == 1 and has(i, k, -1):
                        r, s = rs(i, k, -1)
                        act.wait_ge(pv_ok, b)
                        if has(i, k, -3):
                            r3, s3 = rs(i, k, -3)
                            act.wait_ge(u_out[s3], 16 * (r3 + 1))
                        nc.scalar.copy(u_sb[:, s % 2].rearrange("p f l -> p (f l)"), ps[:, PS_U, :]).then_inc(u_ok, 1)
                    if p == 2 and has(i, k, 1):
                        v_out(i, k, 1)

            steps(act, step)

            def chunk_high(c):
                act.wait_ge(t_ok, c + 1)
                nc.scalar.copy(x_t[:, 0], ps[:, PS_T:PS_T + HT, :]).then_inc(hi_ok, 1)

            chunk_high(0)

            def chunk(c, last):
                for it in range(IT):
                    n = IT * c + it
                    act.wait_ge(gu_ok, n + 1)
                    if it >= 2:
                        act.wait_ge(fu_ok, n - 1)
                    nc.scalar.activation(th[:, it % 2, :], ps[:, PS_GU + 2 * (it % 2), :], ACT.Tanh,
                                         scale=gs_half[:, it:it + 1]).then_inc(th_ok, 1)
                    act.wait_ge(fu_ok, n + 1)
                    nc.scalar.copy(f_hi[:, it, :], fu[:, it % 2, :]).then_inc(fh_ok, 1)
                if not last:
                    chunk_high(c + 1)

            act.wait_ge(coef_ok, 1)
            with act.Fori(0, NCH - 1) as c:
                chunk(c, False)
            chunk(NCH - 1, True)

        @block.vector
        def _(v):
            n_dve = [0]

            def link(ins):
                n_dve[0] += 1
                ins.then_inc(dve, 1)
                v.wait_ge(dve, n_dve[0])

            def stats_half(n):
                tiles = range(HH * n, HH * (n + 1))
                v.wait_ge(x_in[n], 16 * HH)
                for t in tiles:
                    last = nc.vector.bn_stats(stats[:, t, :], x_sb[:, t, :])
                link(last)
                for t in tiles:
                    last = nc.vector.bn_aggr(mv[:, t, :], stats[:, t, :])
                link(last)
                at = slice(HH * n, HH * (n + 1))
                nc.vector.tensor_scalar(veps[:, at], mv[:, at, 1], EPS, None, ALU.add).then_inc(veps_ok, 1)

            def normalise_half(n):
                v.wait_ge(rstd_ok, n + 1)
                if n >= 2:
                    v.wait_ge(q_split0, n - 1)
                for t in range(HH * n, HH * (n + 1)):
                    nc.vector.tensor_scalar(xn[:, t % NH, :], x_sb[:, t, :], mv[:, t, 0:1], rstd[:, t:t + 1],
                                            ALU.subtract, ALU.mult).then_inc(xn_ok, 1)

            def split_half(n):
                at = slice(HH * n, HH * (n + 1))
                v.wait_ge(xn_ok, HH * (n + 1))
                link(nc.vector.tensor_copy(q_parts[:, 0, at, :], xn[:, at, :]))
                link(nc.vector.tensor_tensor(rest_v, xn[:, at, :], q_parts[:, 0, at, :], ALU.subtract))
                link(nc.vector.tensor_copy(q_parts[:, 1, at, :], rest_v))
                nc.vector.tensor_tensor(q_parts[:, 2, at, :], rest_v, q_parts[:, 1, at, :],
                                        ALU.subtract).then_inc(q_split0, 1)

            stats_half(0)
            normalise_half(0)
            stats_half(1)
            split_half(0)
            normalise_half(1)
            v.wait_ge(q_split0, 1)
            split_half(1)
            v.wait_ge(tanh_ok, 1)
            link(nc.vector.tensor_tensor(c_att[:], tanhs[:, 0:1], gates[:, 2:3], ALU.mult))

            def coefficients():
                v.wait_ge(scales_in, 48)
                nc.vector.tensor_scalar(ds_row[:], ds_row[:], tanhs[:, 1:2], None, ALU.mult)
                nc.vector.tensor_scalar(gs_half[:], gs[:], 0.5, None, ALU.mult).then_inc(coef_ok, 1)
                v.wait_ge(coef_ok, 1)
                link(nc.vector.tensor_tensor(gus[:], gs_half[:], us[:], ALU.mult))

            def reduce_max(n, before, h, quad):
                v.wait_ge(s_ok, n + 1)
                if h == 0 and before is not None:
                    v.wait_ge(mt_ok, before)
                nc.vector.tensor_reduce(neg_max[:, quad, LT * h:LT * (h + 1)],
                                        ps[:, PS_S + h % 2, :].rearrange("p (t l) -> p t l", t=LT),
                                        axis=AX.X, op=ALU.max, negate=True).then_inc(max_ok, 1)

            def split_max(i, k, off, quad):
                r, s = rs(i, k, off)
                b = RING * r + s
                v.wait_ge(mt_ok, 2 * b + quad + 1)
                if has(i, k, off - 1):
                    r1, s1 = rs(i, k, off - 1)
                    v.wait_ge(mx_in[quad][s1], 32 * (r1 + 1))
                src = ps[0:QUAD * LT, PS_M, 0:P]
                nc.vector.tensor_copy(max_t[:, quad, 0, :], src).then_inc(mt_hi, 1)
                v.wait_ge(mt_hi, 2 * b + quad + 1)
                nc.vector.tensor_tensor(max_t[:, quad, 1, :], src, max_t[:, quad, 0, :],
                                        ALU.subtract).then_inc(mt_split, 1)

            for idx in range(8):
                reduce_max(idx, None, idx % 4, idx // 4)
                if idx == 5:
                    split_max(0, 0, 0, 0)
            for idx in range(8, 12):
                reduce_max(idx, 1, idx % 4, 0)
                if idx == 9:
                    split_max(0, 0, 0, 1)

            def step(i, k):
                b = RING * i + k
                for n in range(8):
                    if has(i, k, 1 if n < 4 else 2):
                        reduce_max(8 * b + 12 + n, 2 * b + 2 + n // 4, n % 4, 1 if n < 4 else 0)
                    if n == 1 and has(i, k, 1):
                        split_max(i, k, 1, 0)
                    if n == 5 and has(i, k, 1):
                        split_max(i, k, 1, 1)

            def binades(m):
                raw = w_raw[m][:].rearrange("p t n -> p (t n)")
                if m:
                    v.wait_ge(w_ok, m)
                link(nc.vector.tensor_scalar(w_exp.bitcast(u32), raw.bitcast(u32), 0x7F800000, None,
                                             ALU.bitwise_and))
                nc.vector.tensor_scalar(w_exp, w_exp, E4M3_MIN_EXP, E4M3_MAGIC,
                                        ALU.max, ALU.mult).then_inc(w_exp_ok, 1)

            def reciprocals(g):
                v.wait_ge(sum_in[g], 32)
                if g:
                    v.wait_ge(rec_out[g - 1], 32)
                nc.vector.reciprocal(r_sp[:], s_sp[:]).then_inc(rec_ok, 1)

            def add_attention(g, n):
                v.wait_ge(att_ok, 2 * g + n + 1)
                at = slice(HH * n, HH * (n + 1))
                xh = x_sb[:, NH * g + HH * n:NH * g + HH * (n + 1), :].rearrange("p h l -> p (h l)")
                nc.vector.scalar_tensor_tensor(xh, u_n[:, at, :].rearrange("p h l -> p (h l)"), c_att[:, 0:1], xh,
                                               ALU.mult, ALU.add).then_inc(x1_ok, 1)

            def norm_chunk(c):
                v.wait_ge(x1_ok, c + 1)
                for q in range(CH):
                    t = CH * c + q
                    nc.vector.bn_stats(stats[:, q, :], x_sb[:, bass.ds(t, 1), :].rearrange("p a l -> p (a l)")
                                       ).then_inc(n2_stats, 1)
                for q in range(CH):
                    v.wait_ge(n2_stats, CH * c + q + 1)
                    apart(v, 1)
                    nc.vector.bn_aggr(mv[:, q, :], stats[:, q, :]).then_inc(n2_aggr, 1)
                v.wait_ge(n2_aggr, CH * c + CH)
                nc.vector.tensor_scalar(veps[:, bass.ds(CH * c, CH)], mv[:, 0:CH, 1], EPS, None,
                                        ALU.add).then_inc(v2_ok, CH)

            def norm_apply(c):
                v.wait_ge(r2_ok, c + 1)
                if not isinstance(c, int) or c > 0:
                    v.wait_ge(t_ok, c)
                for q in range(CH):
                    t = CH * c + q
                    nc.vector.tensor_scalar(xn2[:, q, :], x_sb[:, bass.ds(t, 1), :].rearrange("p a l -> p (a l)"),
                                            mv[:, q, 0:1], rstd[:, bass.ds(t, 1)],
                                            ALU.subtract, ALU.mult).then_inc(n2_ok, 1)

            def chunk_low(c):
                v.wait_ge(hi_ok, c + 1)
                nc.vector.tensor_tensor(x_t[:, 1], ps[:, PS_T:PS_T + HT, :], x_t[:, 0],
                                        ALU.subtract).then_inc(lo_ok, 1)

            def step_v(i, k):
                if first(i):
                    if k == 0:
                        stats_half(2)
                        stats_half(3)
                    if k == 1:
                        normalise_half(2)
                        normalise_half(3)
                    if k == 3:
                        coefficients()
                if final(i):
                    if k == 0:
                        v.wait_ge(w_in, 48)
                        v.wait_ge(scr_out[2], 96)
                        v.wait_ge(scr_out[3], 96)
                        binades(0)
                    if k == 1:
                        reciprocals(0)
                        binades(1)
                    if k == 2:
                        binades(2)
                    if k == 3:
                        add_attention(0, 0)
                        add_attention(0, 1)
                step(i, k)

            steps(v, step_v)
            norm_chunk(0)
            norm_apply(0)
            chunk_low(0)
            reciprocals(1)

            def chunk(c, last, second=False):
                for it in range(IT):
                    n = IT * c + it
                    v.wait_ge(th_ok, n + 1)
                    nc.vector.scalar_tensor_tensor(ga[:, it % 2, :], th[:, it % 2, :], 1.0,
                                                   ps[:, PS_GU + 2 * (it % 2), :], ALU.add, ALU.mult).then_inc(ga_ok, 1)
                    v.wait_ge(ga_ok, n + 1)
                    if it >= 2 or not isinstance(c, int) or c > 0:
                        v.wait_ge(fl_ok, n - 1)
                    nc.vector.scalar_tensor_tensor(fu[:, it % 2, :], ps[:, PS_GU + 2 * (it % 2) + 1, :],
                                                   gus[:, it:it + 1], ga[:, it % 2, :],
                                                   ALU.mult, ALU.mult).then_inc(fu_ok, 1)
                    if second and it in (4, 5):
                        add_attention(1, it - 4)
                    if it == 1 and not last:
                        norm_chunk(c + 1)
                    if it == 3 and not last:
                        norm_apply(c + 1)
                if not last:
                    chunk_low(c + 1)
                for q in range(CH):
                    t = CH * c + q
                    n = q % 2
                    v.wait_ge(y_ok, t + 1)
                    nc.vector.tensor_tensor(yo[:, n, :], ps[:, PS_Y + n, 0:L], ds_row[:], ALU.mult).then_inc(yo_ok, 1)
                    v.wait_ge(yo_ok, t + 1)
                    if q >= 2 or not isinstance(c, int) or c > 0:
                        v.wait_ge(out_ok[n], 16 * (2 * c + q // 2))
                    nc.vector.tensor_tensor(o_sb[:, n, :], yo[:, n, :],
                                            x_sb[:, bass.ds(t, 1), :].rearrange("p a l -> p (a l)"),
                                            ALU.add).then_inc(o_ok, 1)

            chunk(0, False, True)
            with v.Fori(1, NCH - 1) as c:
                chunk(c, False)
            chunk(NCH - 1, True)

        @block.tensor
        def _(pe):
            def scores(idx, r, s, h):
                if not isinstance(idx, int) or idx >= 2:
                    pe.wait_ge(max_ok, idx - 1)
                for t in range(LT):
                    last = nc.tensor.matmul(ps[:, PS_S + h % 2, L * t:L * (t + 1)],
                                            q_st[0:KS, s, h, P * t:P * (t + 1)], k_st[0:KS, s, h, :],
                                            start=True, stop=True)
                last.then_inc(s_ok, 1)

            def scores_t(i, k, p):
                b = RING * i + k
                if p % 2 == 0:
                    pe.wait_ge(mx_in[p // 2][k], 32 * (i + 1))
                if p >= 2 or has(i, k, -1):
                    pe.wait_ge(exp_ok, 4 * b + p - 1)
                for m in range(2):
                    h = 2 * p + m
                    for t in range(LT):
                        last = nc.tensor.matmul(ps[:, PS_ST + 2 * (p % 2) + m, L * t:L * (t + 1)],
                                                k_st[0:KS + MAXROWS, k, h, P * t:P * (t + 1)],
                                                q_st[0:KS + MAXROWS, k, h, :], start=True, stop=True)
                last.then_inc(st_ok, 1)

            def transpose_max(i, k, off, quad):
                r, s = rs(i, k, off)
                b = RING * r + s
                pe.wait_ge(max_ok, 8 * b + 4 * (quad + 1))
                if quad == 0:
                    if has(i, k, off - 1):
                        pe.wait_ge(mt_split, 2 * b)
                    pe.wait_ge(vt_sb, b if has(i, k, off - 1) else 1)
                else:
                    pe.wait_ge(mt_split, 2 * b + 1)
                    pe.wait_ge(vt_sb, b + 1)
                nc.tensor.transpose(ps[0:QUAD * LT, PS_M, 0:P], neg_max[:, quad, :], ident[:]).then_inc(mt_ok, 1)

            def transpose_ctx(i, k, off):
                r, s = rs(i, k, off)
                b = RING * r + s
                pe.wait_ge(ctx_in[s], 16 * (r + 1))
                if has(i, k, off - 1):
                    pe.wait_ge(mt_split, 2 * b + 1)
                for t in range(LT):
                    last = nc.tensor.transpose(ps[:, PS_M, P * t:P * (t + 1)], ctx_t[:, s, P * t:P * (t + 1)], ident[:])
                last.then_inc(vt_ok, 1)

            def weighted(i, k, off, quad):
                r, s = rs(i, k, off)
                b = RING * r + s
                pe.wait_ge(exp_ok, 4 * b + 2 * (quad + 1))
                if quad == 0:
                    pe.wait_ge(vt_sb, b + 1)
                    if has(i, k, off - 1):
                        pe.wait_ge(u_ok, b)
                for t in range(LT):
                    for j in range(QUAD):
                        h = QUAD * quad + j
                        last = nc.tensor.matmul(ps[32 * j:32 * (j + 1), PS_U, L * quad:L * (quad + 1)],
                                                v_t[:, s % 2, t, h, :], p_t[:, s % 2, h, L * t:L * (t + 1)],
                                                start=(t == 0), stop=(t == LT - 1))
                if quad == 1:
                    last.then_inc(pv_ok, 1)

            pe.wait_ge(consts, 2)
            transpose_ctx(0, 0, 0)
            pe.wait_ge(st_in[0], 16)
            for idx in range(8):
                scores(idx, 0, 0, idx)
                if idx == 5:
                    transpose_max(0, 0, 0, 0)
            pe.wait_ge(st_in[1], 16)
            for idx in range(8, 12):
                scores(idx, 0, 1, idx - 8)
                if idx == 9:
                    transpose_max(0, 0, 0, 1)
            pe.wait_ge(ones_set, 1)

            def step(i, k):
                b = RING * i + k
                for p in range(4):
                    if has(i, k, 0):
                        scores_t(i, k, p)
                    off = 1 if p < 2 else 2
                    if has(i, k, off):
                        r, s = rs(i, k, off)
                        if p == 2:
                            pe.wait_ge(st_in[s], 16 * (r + 1))
                        for m in range(2):
                            n = 2 * p + m
                            scores(8 * b + 12 + n, r, s, (n + 4) % 8)
                    if p == 0 and has(i, k, 1):
                        transpose_max(i, k, 1, 0)
                    if p == 0 and has(i, k, -1):
                        weighted(i, k, -1, 1)
                    if p == 1 and has(i, k, 1):
                        transpose_ctx(i, k, 1)
                    if p == 2 and has(i, k, 1):
                        transpose_max(i, k, 1, 1)
                    if p == 2 and has(i, k, 0):
                        weighted(i, k, 0, 0)

            steps(pe, step)

            def transposes(c):
                pe.wait_ge(n2_ok, CH * (c + 1))
                for q in range(CH):
                    for ht in range(HT):
                        last = nc.tensor.transpose(ps[:, PS_T + ht, P * q:P * (q + 1)],
                                                   xn2[:, q, P * ht:P * (ht + 1)], ident[:])
                last.then_inc(t_ok, 1)

            def gate_up(c):
                pe.wait_ge(lo_ok, c + 1)
                for it in range(IT):
                    n = IT * c + it
                    if it >= 2 or not isinstance(c, int) or c > 0:
                        pe.wait_ge(fu_ok, n - 1)
                    for m, w in enumerate((wg, wu)):
                        for j in range(2 * HT):
                            ht, part = j // 2, j % 2
                            last = nc.tensor.matmul(ps[:, PS_GU + 2 * (it % 2) + m, :], w[:, ht, P * it:P * (it + 1)],
                                                    x_t[:, part, ht, :], start=(j == 0), stop=(j == 2 * HT - 1))
                    last.then_inc(gu_ok, 1)

            def down(c):
                pe.wait_ge(fl_ok, IT * (c + 1))
                for q in range(CH):
                    t = CH * c + q
                    if q >= 2 or not isinstance(c, int) or c > 0:
                        pe.wait_ge(yo_ok, t - 1)
                    for j in range(2 * IT):
                        it, f = j // 2, (f_hi, f_lo)[j % 2]
                        last = nc.tensor.matmul(ps[:, PS_Y + q % 2, 0:L], f[:, it, P * q:P * (q + 1)],
                                                wd[:, it, :], start=(j == 0), stop=(j == 2 * IT - 1))
                    last.then_inc(y_ok, 1)

            pe.wait_ge(u_ok, NB)
            pe.wait_ge(mt_split, 2 * NB)
            transposes(0)
            pe.wait_ge(w_ok, 3)

            def chunk(c, last):
                gate_up(c)
                if not last:
                    transposes(c + 1)
                down(c)

            chunk(0, False)
            with pe.Fori(1, NCH - 1) as c:
                chunk(c, False)
            chunk(NCH - 1, True)


_INS = ["x", "ctx_2048", "g_xattn", "g_ffn", "L0_xattn_gamma", "L0_ffn_gate_w", "L0_ffn_up_w", "L0_ffn_down_w",
        "L0_ffn_gate_scale", "L0_ffn_up_scale", "L0_ffn_down_scale"]


def kernel(**inputs):
    import numpy as np
    import concourse.bacc as bacc
    from concourse import mybir
    from concourse.bass_utils import run_bass_kernel_spmd

    nc = bacc.Bacc("TRN2", target_bir_lowering=False, num_devices=1)
    arrays, args = {}, []
    for name in _INS:
        a = np.ascontiguousarray(inputs[name])
        if a.ndim == 0:
            a = a.reshape(1)
        arrays[f"in_{name}"] = a
        args.append(nc.dram_tensor(f"in_{name}", a.shape, mybir.dt.from_np(a.dtype), kind="ExternalInput").ap())
    shape = (NB, D, L)
    result = nc.dram_tensor("out_x", shape, mybir.dt.float32, kind="ExternalOutput").ap()
    build(nc, *args, result)
    r = run_bass_kernel_spmd(nc, [arrays], core_ids=[0])
    return r.results[0]["out_x"]
```

```python
import concourse.bass as bass
from concourse import mybir
from contextlib import ExitStack

NB = 16
D = 128
L = 256
NH = 8
DH = D // NH
P = 128
LT = L // P
NPART = 3
GB = P // DH
NG = NB // GB
HH = NH // 2
NPROD = 6
RUNS = [(0, 3, 0), (3, 2, 1), (5, 1, 2)]
KS = DH * NPROD
SAVES = [(0, 0, 8), (1, 0, 4), (1, 4, 8), (2, 0, 8), (3, 0, 8)]
MAXROWS = 2
RING = 4
QUAD = 4
SLOTW = 32
I = 768
IT = I // P
HT = L // P
CH = 4
NCH = NB // CH
TOK = CH * P
EPS = 1e-5
E4M3_MIN_EXP = 2.0 ** -6
E4M3_MAGIC = 1.5 * 2.0 ** 20


def build(nc, x, ctx, g_xattn, g_ffn, gamma, gate_w, up_w, down_w, gate_scale, up_scale, down_scale, out):
    f32, f32r, bf16, f16, u32 = (mybir.dt.float32, mybir.dt.float32r, mybir.dt.bfloat16,
                                 mybir.dt.float16, mybir.dt.uint32)
    ALU = mybir.AluOpType
    ACT = mybir.ActivationFunctionType
    AX = mybir.AxisListType

    es = ExitStack()
    with es:
        def sb(name, shape, dt=f32):
            return es.enter_context(nc.sbuf_tensor(name, shape, dt))

        def sem(name):
            return es.enter_context(nc.semaphore(name))

        def sems(name, n=RING):
            return [sem(f"{name}{j}") for j in range(n)]

        parts_scr = nc.dram_tensor("parts_scr", (2, NB, DH, NPART, NH, L), bf16, kind="Internal").ap()
        u_scr = nc.dram_tensor("u_scr", (NB, QUAD, P // QUAD, 2, L), f32, kind="Internal").ap()
        r_scr = nc.dram_tensor("r_scr", (NB, 2, QUAD, L), f32, kind="Internal").ap()

        ident = sb("ident", [P, P])
        ident_b = sb("ident_b", [P, P], bf16)
        x_sb = sb("x_sb", [P, NG * NH, L])
        c_sb = sb("c_sb", [P, NG * NH, L])
        xn = sb("xn", [P, NH, L])
        rest = sb("rest", [P, HH, L])
        parts = sb("parts", [P, 2, NPART, NH, L], bf16)
        ctx_t = sb("ctx_t", [P, RING, L])
        st = sb("st", [P, RING, 2, NH, L], bf16)
        q_st, k_st = st[:, :, 0], st[:, :, 1]
        neg_max = sb("neg_max", [P, 2, NH * LT])
        max_parts = sb("max_parts", [P, MAXROWS, NH * LT], bf16)
        max_t = sb("max_t", [MAXROWS * NH * LT, P], bf16)
        p_t = sb("p_t", [P, 2, NH, LT * L])
        rest_v = p_t[:, 1, 0:2, :].rearrange("p a l -> p (a l)").rearrange("p (h l) -> p h l", h=HH)
        v_t = sb("v_t", [P, 2, LT, NH, SLOTW])
        u_sb = sb("u_sb", [P, 2, 2, L])
        s_sp = sb("s_sp", [P, GB * NH * L // P])
        r_sp = sb("r_sp", [P, GB * NH * L // P])
        u_n, r_n = c_sb[:, 0:NH, :], c_sb[:, NH:2 * NH, :]
        stats = sb("stats", [P, NB, 6])
        mv = sb("mv", [P, NB, 2])
        veps = sb("veps", [P, NB])
        rstd = sb("rstd", [P, NB])
        mhalf = sb("mhalf", [P, NB])
        gates = sb("gates", [P, 3])
        tanhs = sb("tanhs", [P, 2])
        c_att = sb("c_att", [P, 1])
        gs = sb("gs", [P, IT])
        us = sb("us", [P, IT])
        gs_half = sb("gs_half", [P, IT])
        gus = sb("gus", [P, IT])
        ds_row = sb("ds_row", [P, L])
        w_all = sb("w_all", [P, 3, HT * I])
        held = parts[:].rearrange("p m c h l -> p (m c h l)")
        x_t = held[:, 0:NCH * 2 * HT * TOK].bitcast(f16).rearrange("p (c a t n) -> p c a t n", c=NCH, a=2, t=HT)
        w_exp = held[:, held.shape[1] - 3 * 2 * HT * I:].bitcast(f32).rearrange("p (m n) -> p m n", m=3)
        w_gu = sb("w_gu", [P, 2, HT * I], f16)
        wg, wu = (w_gu[:, m].rearrange("p (t n) -> p t n", t=HT) for m in range(2))
        wd = sb("wd", [P, IT, L], f32r)
        def as_parts(ap):
            return ap.bitcast(bf16).rearrange("p (c h l) -> p c h l", c=NPART, h=HH)
        q_parts, k_parts = ([parts[:, m, :, 0:HH], parts[:, m, :, HH:NH]] for m in range(2))
        k_parts += [as_parts(w_all[:, n]) for n in range(2)]
        q_parts += [as_parts(w_all[:, 2]), as_parts(w_gu[:].rearrange("p m n -> p (m n)"))]
        xn2 = xn[:, 0:CH, :]
        NBUF = 2
        th, ga, fu = (p_t[:, 0, 2 * m:2 * m + 2, :] for m in range(3))
        f_hi = sb("f_hi", [P, IT, TOK], f32r)
        f_lo = sb("f_lo", [P, IT, TOK], f32r)
        yo, o_sb = (p_t[:, 1, 2 * NBUF * m:2 * NBUF * (m + 1), :] for m in range(2))
        zeros = sb("zeros", [1, TOK], f16)
        ps = es.enter_context(nc.psum_tensor("ps", [P, 8, 512], f32))
        PS_S, PS_ST, PS_U, PS_M = 0, 4, 6, 7
        NSB, NTB = 4, 2
        PS_GU, PS_T, PS_Y = 0, 4, 6
        PS_T0 = 2
        WD = 2

        x_in = sems("x_in", 2 * NG)
        c_in = sems("c_in", 2 * NG)
        ctx_in = sems("ctx_in")
        gates_in = sem("gates_in")
        scales_in = sem("scales_in")
        w_in = sems("w_in", 3)
        consts = sem("consts")
        ones_set = sem("ones_set")
        veps_ok = sem("veps_ok")
        rstd_ok = sem("rstd_ok")
        tanh_ok = sem("tanh_ok")
        coef_ok = sem("coef_ok")
        xn_ok = sem("xn_ok")
        q_split = sem("q_split")
        q_hi = sem("q_hi")
        q_rest = sem("q_rest")
        q_last = sem("q_last")
        k_hi = sem("k_hi")
        k_rest = sem("k_rest")
        k_split = sem("k_split")
        scr_out = sems("scr_out", len(SAVES))
        q_in = sems("q_in")
        k_in = sems("k_in")
        k_first = sems("k_first", 2)
        mx_in = sems("mx_in")
        s_ok = sem("s_ok")
        max_ok = sem("max_ok")
        mx_hi = sem("mx_hi")
        mx_split = sem("mx_split")
        mt_ok = sem("mt_ok")
        mt_sb = sem("mt_sb")
        st_ok = sem("st_ok")
        exp_ok = sem("exp_ok")
        vt_ok = sem("vt_ok")
        vt_sb = sem("vt_sb")
        pv_ok = sem("pv_ok")
        u_ok = sem("u_ok")
        u_out = sems("u_out")
        u_in = sems("u_in", 2 * NG)
        sum_in = sems("sum_in", NG)
        rec_ok = sem("rec_ok")
        rec_out = sems("rec_out", NG)
        rec_in = sems("rec_in", 2 * NG)
        att_ok = sem("att_ok")
        x1_ok = sem("x1_ok")
        dve = sem("dve_order")
        pool_o = sem("pool_order")
        taken = sem("taken")
        w_exp_ok = sem("w_exp_ok")
        w_and = sem("w_and")
        w_sum = sem("w_sum")
        w_ok = sem("w_ok")
        v2_ok = sem("v2_ok")
        r2_ok = sem("r2_ok")
        n2_ok = sem("n2_ok")
        t_ok = sem("t_ok")
        hi_ok = sem("hi_ok")
        lo_ok = sem("lo_ok")
        gu_ok = sem("gu_ok")
        th_ok = sem("th_ok")
        fu_ok = sem("fu_ok")
        fh_ok = sem("fh_ok")
        fl_ok = sem("fl_ok")
        fl_last = sem("fl_last")
        y_ok = sem("y_ok")
        o_ok = sem("o_ok")
        last_ok = sem("last_ok")
        out_ok = sem("out_ok")
        n2_stats = sem("n2_stats")
        n2_aggr = sem("n2_aggr")
        ga_ok = sem("ga_ok")
        yo_ok = sem("yo_ok")

        def buffer(of, c):
            slot = c % NBUF if isinstance(c, int) else c
            return of[:, bass.ds(2 * slot, 2), :].rearrange("p a n -> p (a n)")

        block = es.enter_context(nc.Block())

        def load_half(eng, src, dst, done, n):
            g = n // 2
            for h in range(HH * (n % 2), HH * (n % 2 + 1)):
                eng.dma_start(dst[:, NH * g + h, :], src[GB * g:GB * (g + 1), DH * h:DH * (h + 1), :]
                              ).then_inc(done[n], 16)

        def load_stack(eng, b, s, m, done):
            for c, count, part in RUNS:
                first_part, nparts = (0, count) if m else (part, 1)
                src = parts_scr[m, bass.ds(b, 1), :, first_part:first_part + nparts].rearrange(
                    "a d c h l -> (a c) d (h l)")
                if nparts < count:
                    src = src.broadcast_to([count, DH, NH * L])
                eng.dma_start(st[DH * c:DH * (c + count), s, m].rearrange("p h l -> p (h l)"), src
                              ).then_inc(done, 16)

        STACK = 16 * len(RUNS)

        def slot_free(eng, i, k):
            if has(i, k, -1):
                eng.wait_ge(st_ok, NH * (RING * i + k))

        def saved(eng, i, k):
            if first(i):
                for n in {0: (2,), 1: (3,), 3: (4,)}.get(k, ()):
                    eng.wait_ge(scr_out[n], 32)

        def has(i, k, off):
            return not isinstance(i, int) or 0 <= RING * i + k + off < NB

        def apart(eng):
            eng.sem_inc(taken, 1)

        def first(i):
            return isinstance(i, int) and i == 0

        def final(i):
            return isinstance(i, int) and i == NB // RING - 1

        def rs(i, k, off):
            return i + (k + off) // RING, (k + off) % RING

        def steps(eng, step):
            for k in range(RING):
                step(0, k)
            with eng.Fori(1, NB // RING - 1) as i:
                for k in range(RING):
                    step(i, k)
            for k in range(RING):
                step(NB // RING - 1, k)
            step(NB // RING, 0)

        @block.sync
        def _(sp):
            def load_ctx(b, slot):
                sp.dma_start(ctx_t[:, slot, :], ctx[bass.ds(b, 1)].rearrange("a p l -> (a p) l")
                             ).then_inc(ctx_in[slot], 16)

            def save(n):
                half, b0, b1 = SAVES[n]
                g, h = half // 2, HH * (half % 2)
                for m, src, done, count in ((0, q_parts[half], *((q_last, 1) if half == 3 else (q_split, half + 1))),
                                            (1, k_parts[half], k_split, half + 1)):
                    sp.wait_ge(done, count)
                    dst = parts_scr[m, GB * g + b0:GB * g + b1, :, :, h:h + HH, :].rearrange(
                        "b d c h l -> (b d) c (h l)")
                    sp.dma_start(dst, src[DH * b0:DH * b1].rearrange("p c h l -> p c (h l)")).then_inc(scr_out[n], 16)

            def load_maxima(i, k, off):
                r, s = rs(i, k, off)
                sp.wait_ge(mt_sb, RING * r + s + 1)
                sp.dma_start(q_st[KS:KS + MAXROWS, s].rearrange("p h l -> p (h l)"), max_t[:]).then_inc(mx_in[s], 16)

            load_half(sp, x, x_sb, x_in, 0)
            load_half(sp, ctx, c_sb, c_in, 1)
            load_half(sp, x, x_sb, x_in, 1)
            load_ctx(0, 0)
            for dst, src in ((gates[:, 0:1], g_xattn), (gates[:, 1:2], g_ffn), (gates[:, 2:3], gamma)):
                sp.dma_start(dst, src.rearrange("(a c) -> a c", c=1).broadcast_to([P, 1])).then_inc(gates_in, 16)
            load_half(sp, ctx, c_sb, c_in, 2)
            load_half(sp, x, x_sb, x_in, 2)
            save(0)
            load_half(sp, ctx, c_sb, c_in, 3)
            load_half(sp, x, x_sb, x_in, 3)
            save(1)
            for n in range(2):
                sp.wait_ge(scr_out[n], 32)
            load_stack(sp, 0, 0, 0, q_in[0])
            load_stack(sp, 0, 0, 1, k_first[0])
            save(2)
            load_stack(sp, 1, 1, 0, q_in[1])
            load_stack(sp, 1, 1, 1, k_first[1])
            load_stack(sp, 2, 2, 0, q_in[2])
            load_ctx(1, 1)
            load_maxima(0, 0, 0)
            save(3)
            for b in range(2, RING):
                load_ctx(b, b)

            def load_sums(g):
                for b in range(GB * g, GB * (g + 1)):
                    sp.wait_ge(u_out[b % RING], 16 * (b // RING + 1))
                for half in range(2):
                    sp.dma_start(s_sp[P // 2 * half:P // 2 * (half + 1), :], u_scr[GB * g:GB * (g + 1), :, 0, half, :]
                                 ).then_inc(sum_in[g], 16)

            def load_heads(g, half):
                if half == 0:
                    if g:
                        sp.wait_ge(x1_ok, 2)
                    else:
                        sp.wait_ge(k_split, 2 * NG)
                for j in range(QUAD):
                    sp.dma_start(u_n[:, QUAD * half + j, :], u_scr[GB * g:GB * (g + 1), j, 1:1 + DH, half, :]
                                 ).then_inc(u_in[2 * g + half], 16)

            def save_reciprocals(g):
                sp.wait_ge(rec_ok, g + 1)
                for half in range(2):
                    sp.dma_start(r_scr[GB * g:GB * (g + 1), half].rearrange("b j l -> b (j l)"),
                                 r_sp[P // 2 * half:P // 2 * (half + 1), :]).then_inc(rec_out[g], 16)

            def load_reciprocals(g, half):
                if half == 0:
                    sp.wait_ge(rec_out[g], 32)
                src = r_scr[GB * g:GB * (g + 1), half].rearrange("b j l -> b (j l)")
                src = src.rearrange("b (a n) -> b a n", a=1).broadcast_to([GB, DH, HH * L])
                sp.dma_start(r_n[:, HH * half:HH * (half + 1), :].rearrange("p h l -> p (h l)"), src
                             ).then_inc(rec_in[2 * g + half], 16)

            def step(i, k):
                b = RING * i + k
                if final(i) and k == 0:
                    load_sums(0)
                if has(i, k, 3):
                    slot_free(sp, i, k)
                    load_stack(sp, b + 3, (k + 3) % RING, 0, q_in[(k + 3) % RING])
                if has(i, k, 1):
                    load_maxima(i, k, 1)
                if has(i, k, -1):
                    r, s = rs(i, k, -1)
                    sp.wait_ge(u_ok, b)
                    sp.dma_start(u_scr[bass.ds(b - 1, 1)].rearrange("a j r f l -> (a j r) (f l)"),
                                 u_sb[:, s % 2].rearrange("p f l -> p (f l)")).then_inc(u_out[s], 16)
                if has(i, k, 4):
                    sp.wait_ge(vt_ok, b + 1)
                    load_ctx(b + 4, k)
                if first(i) and k == 0:
                    save(4)
                saved(sp, i, k)
                if final(i) and k == 0:
                    load_heads(0, 0)
                    save_reciprocals(0)
                if final(i) and k == 1:
                    load_reciprocals(0, 0)
                    load_heads(0, 1)
                if final(i) and k == 2:
                    load_reciprocals(0, 1)

            steps(sp, step)

            load_sums(1)
            load_heads(1, 0)
            save_reciprocals(1)
            load_heads(1, 1)
            load_reciprocals(1, 0)
            load_reciprocals(1, 1)

            def store(c):
                g, h = CH * c // NH, CH * c % NH
                if c < NCH - 2:
                    sp.wait_ge(o_ok, c + 1)
                for q in range(CH):
                    if c >= NCH - 2:
                        sp.wait_ge(last_ok, 1 if c < NCH - 1 else 2 + q // 2)
                    src = buffer(o_sb, c)[:, L * q:L * (q + 1)]
                    sp.dma_start(out[GB * g:GB * (g + 1), DH * (h + q):DH * (h + q + 1), :], src).then_inc(out_ok, 16)

            for c in range(NCH):
                store(c)
            sp.wait_ge(out_ok, 16 * NB)

        @block.gpsimd
        def _(pool):
            n_pool = [0]

            def link(ins):
                n_pool[0] += 1
                ins.then_inc(pool_o, 1)
                pool.wait_ge(pool_o, n_pool[0])

            load_half(pool, ctx, c_sb, c_in, 0)
            link(nc.gpsimd.memset(v_t[:].rearrange("p a t h c -> p (a t h c)"), 0.0))
            nc.gpsimd.memset(v_t[:].rearrange("p a t h c -> p (a t h) c")[:, :, 0:1], 1.0).then_inc(consts, 1)
            link(nc.gpsimd.memset(ident[:], 0.0))
            nc.gpsimd.affine_select(out=ident[:], in_=ident[:], compare_op=ALU.not_equal, fill=1.0, base=0,
                                    pattern=[[-1, P]], channel_multiplier=1).then_inc(consts, 1)
            link(nc.gpsimd.memset(ident_b[:], 0.0))
            nc.gpsimd.affine_select(out=ident_b[:], in_=ident_b[:], compare_op=ALU.not_equal, fill=1.0, base=0,
                                    pattern=[[-1, P]], channel_multiplier=1).then_inc(consts, 1)
            nc.gpsimd.memset(mhalf[:], -0.5).then_inc(consts, 1)
            nc.gpsimd.memset(zeros[:], 0.0).then_inc(consts, 1)
            pool.wait_ge(consts, 5)
            def rstd_half(n):
                pool.wait_ge(veps_ok, n + 1)
                at = slice(HH * n, HH * (n + 1))
                nc.gpsimd.tensor_tensor(rstd[:, at], veps[:, at], mhalf[:, at], ALU.pow).then_inc(rstd_ok, 1)

            def heads(n):
                return slice(HH * (n % 2), HH * (n % 2 + 1))

            def flat(ap):
                return ap.rearrange("p h l -> p (h l)")

            def k_low(n):
                k, part = flat(c_sb[:, HH * n:HH * (n + 1), :]), k_parts[n]
                pool.wait_ge(k_hi, 2 * n + 1)
                pool.wait_ge(c_in[n], 16 * HH)
                if n:
                    pool.wait_ge(k_split, n)
                if n == 0:
                    rstd_half(n)
                nc.gpsimd.tensor_tensor(flat(rest[:]), k, flat(part[:, 0]), ALU.subtract).then_inc(k_rest, 1)
                if n:
                    rstd_half(n)
                pool.wait_ge(k_hi, 2 * n + 2)
                nc.gpsimd.tensor_tensor(flat(part[:, 2]), flat(rest[:]), flat(part[:, 1]),
                                        ALU.subtract).then_inc(k_split, 1)

            for n in range(2 * NG):
                k_low(n)
            pool.wait_ge(q_hi, 1)
            pool.wait_ge(k_split, 2 * NG)
            part = q_parts[3]
            nc.gpsimd.tensor_tensor(flat(rest[:]), flat(xn[:, heads(3), :]), flat(part[:, 0]),
                                    ALU.subtract).then_inc(q_rest, 1)
            for n in range(2):
                pool.wait_ge(scr_out[n], 32)
            load_stack(pool, 2, 2, 1, k_in[2])
            pool.wait_ge(q_hi, 2)
            nc.gpsimd.tensor_tensor(flat(part[:, 2]), flat(rest[:]), flat(part[:, 1]),
                                    ALU.subtract).then_inc(q_last, 1)

            def rounded(m, half):
                raw, exp = (a[:, bass.ds(m, 1), :].rearrange("p a n -> p (a n)") for a in (w_all, w_exp))
                to = wd[:].rearrange("p t n -> p (t n)")
                if m is not WD:
                    to = w_gu[:, bass.ds(m, 1), :].rearrange("p a n -> p (a n)")
                if not half:
                    pool.wait_ge(w_exp_ok, m + 1)
                    nc.gpsimd.tensor_tensor(raw, raw, exp, ALU.add).then_inc(w_sum, 1)
                else:
                    pool.wait_ge(w_sum, m + 1)
                    nc.gpsimd.tensor_tensor(to, raw, exp, ALU.subtract).then_inc(w_ok, 1)

            def attention(g, n):
                pool.wait_ge(u_in[2 * g + n], 16 * HH)
                pool.wait_ge(rec_in[2 * g + n], 16)
                u = flat(u_n[:, heads(n), :])
                nc.gpsimd.tensor_tensor(u, u, flat(r_n[:, heads(n), :]), ALU.mult).then_inc(att_ok, 1)

            def rstd_chunk(c):
                pool.wait_ge(v2_ok, CH * (c + 1))
                nc.gpsimd.tensor_tensor(rstd[:, bass.ds(CH * c, CH)], veps[:, bass.ds(CH * c, CH)],
                                        mhalf[:, 0:CH], ALU.pow).then_inc(r2_ok, 1)

            def load_weight(m, w):
                src = w.rearrange("(t p) n -> p t n", p=P)
                pool.dma_start(w_all[:, m].rearrange("p (t n) -> p t n", t=src.shape[1]), src).then_inc(w_in[m], 16)

            def step(i, k):
                b = RING * i + k
                if has(i, k, 3):
                    slot_free(pool, i, k)
                    load_stack(pool, b + 3, (k + 3) % RING, 1, k_in[(k + 3) % RING])
                saved(pool, i, k)
                if first(i) and k > 0:
                    m = {1: 0, 2: WD, 3: 1}[k]
                    load_weight(m, (gate_w, up_w, down_w)[m])
                if final(i):
                    if k == 0:
                        for dst, src in ((gs, gate_scale), (us, up_scale)):
                            pool.dma_start(dst[:], src.rearrange("(t p) -> p t", p=P),
                                           allow_slow_non_contiguous=True).then_inc(scales_in, 16)
                        pool.dma_start(ds_row[:], down_scale.rearrange("(a c) -> a c", a=1).broadcast_to([P, L])
                                       ).then_inc(scales_in, 16)
                if not isinstance(i, int) and k in (1, 3):
                    rounded(i - 1, k // 2)
                if final(i) and k == 0:
                    rounded(WD, 0)
                    rounded(WD, 1)
                if final(i) and k == 1:
                    attention(0, 0)
                if final(i) and k == 2:
                    rstd_chunk(0)
                    attention(0, 1)
                    rstd_chunk(1)

            steps(pool, step)

            def result(c):
                pool.wait_ge(yo_ok, c + 1)
                x1 = x_sb[:, bass.ds(CH * c, CH), :].rearrange("p h l -> p (h l)")
                nc.gpsimd.tensor_tensor(buffer(o_sb, c), buffer(yo, c), x1, ALU.add).then_inc(o_ok, 1)

            def chunk(c, start, last):
                for it in range(IT):
                    if last and it == IT - 1:
                        break
                    n = IT * c + it
                    pool.wait_ge(fh_ok, n + 1)
                    nc.gpsimd.tensor_tensor(f_lo[:, it, :], fu[:, it % 2, :], f_hi[:, it, :].bitcast(f32),
                                            ALU.subtract).then_inc(fl_ok, 1)
                    if it == 1 and not start and not last:
                        rstd_chunk(c + 1)
                    if it == 3 and not start and not last:
                        result(c - 1)
                    if start and it == 3:
                        attention(1, 0)
                    if start and it == IT - 1:
                        attention(1, 1)

            chunk(0, True, False)
            with pool.Fori(1, NCH - 1) as c:
                chunk(c, False, False)
            chunk(NCH - 1, False, True)

        @block.scalar
        def _(act):
            for n in range(2 * NG):
                at, part = slice(HH * n, HH * (n + 1)), k_parts[n]
                act.wait_ge(c_in[n], 16 * HH)
                nc.scalar.copy(part[:, 0], c_sb[:, at, :]).then_inc(k_hi, 1)
                act.wait_ge(k_rest, n + 1)
                nc.scalar.copy(part[:, 1], rest[:]).then_inc(k_hi, 1)
            act.wait_ge(gates_in, 48)
            nc.scalar.activation(tanhs[:], gates[:, 0:2], ACT.Tanh).then_inc(tanh_ok, 1)

            def v_out(i, k, off):
                r, s = rs(i, k, off)
                b = RING * r + s
                act.wait_ge(vt_ok, b + 1)
                act.wait_ge(consts, 5)
                if has(i, k, off - 2):
                    act.wait_ge(pv_ok, b - 1)
                src = ps[:, PS_M, 0:LT * P].rearrange("p (t h d) -> p t h d", t=LT, h=NH)
                nc.scalar.copy(v_t[:, s % 2, :, :, 1:1 + DH], src).then_inc(vt_sb, 1)

            def chunk_high(c, bank=PS_T):
                act.wait_ge(t_ok, c + 1)
                nc.scalar.copy(x_t[:, bass.ds(c, 1), 0].rearrange("p c t n -> p (c t) n"),
                               ps[:, bank:bank + HT, :]).then_inc(hi_ok, 1)

            v_out(0, 0, 0)
            part = q_parts[3]
            act.wait_ge(xn_ok, NH * NG)
            nc.scalar.copy(part[:, 0], xn[:, HH:NH, :]).then_inc(q_hi, 1)
            act.wait_ge(q_rest, 1)
            nc.scalar.copy(part[:, 1], rest[:]).then_inc(q_hi, 1)

            def step(i, k):
                b = RING * i + k
                for h in range(NH):
                    if has(i, k, 0):
                        act.wait_ge(st_ok, NH * b + h + 1)
                        if h == 0 and has(i, k, -2):
                            act.wait_ge(pv_ok, b - 1)
                        nc.scalar.activation(p_t[:, k % 2, h, :], ps[:, PS_ST + h % NTB, :], ACT.Exp,
                                             scale=DH ** -0.5).then_inc(exp_ok, 1)
                    if h == 3 and has(i, k, -1):
                        r, s = rs(i, k, -1)
                        act.wait_ge(pv_ok, b)
                        if has(i, k, -3):
                            r3, s3 = rs(i, k, -3)
                            act.wait_ge(u_out[s3], 16 * (r3 + 1))
                        nc.scalar.copy(u_sb[:, s % 2].rearrange("p f l -> p (f l)"), ps[:, PS_U, :]).then_inc(u_ok, 1)
                    if h == 6 and has(i, k, 1):
                        v_out(i, k, 1)
                    if final(i) and k == RING - 1 and h == 7:
                        chunk_high(0, PS_T0)

            steps(act, step)

            def gate_tanh(n, it, start):
                act.wait_ge(gu_ok, n + 1)
                if not start:
                    act.wait_ge(ga_ok, n - 1)
                nc.scalar.activation(th[:, it % 2, :], ps[:, PS_GU + 2 * (it % 2), :], ACT.Tanh,
                                     scale=gs_half[:, it:it + 1]).then_inc(th_ok, 1)

            def fused_high(n, it):
                act.wait_ge(fu_ok, n + 1)
                nc.scalar.copy(f_hi[:, it, :], fu[:, it % 2, :]).then_inc(fh_ok, 1)

            def chunk(c, start, last):
                for it in range(IT):
                    n = IT * c + it
                    gate_tanh(n, it, start and it < 2)
                    if it > 0 or not start:
                        fused_high(n - 1, (it - 1) % IT)
                    if it == 4 and not last:
                        chunk_high(c + 1)

            act.wait_ge(coef_ok, 1)
            chunk(0, True, False)
            with act.Fori(1, NCH - 1) as c:
                chunk(c, False, False)
            chunk(NCH - 1, False, True)
            fused_high(IT * NCH - 1, IT - 1)

        @block.vector
        def _(v):
            n_dve = [0]

            def link(ins):
                n_dve[0] += 1
                ins.then_inc(dve, 1)
                v.wait_ge(dve, n_dve[0])

            def stats_half(n):
                tiles = range(HH * n, HH * (n + 1))
                v.wait_ge(x_in[n], 16 * HH)
                for t in tiles:
                    last = nc.vector.bn_stats(stats[:, t, :], x_sb[:, t, :])
                link(last)
                for t in tiles:
                    last = nc.vector.bn_aggr(mv[:, t, :], stats[:, t, :])
                link(last)
                at = slice(HH * n, HH * (n + 1))
                nc.vector.tensor_scalar(veps[:, at], mv[:, at, 1], EPS, None, ALU.add).then_inc(veps_ok, 1)

            def normalise_half(n):
                v.wait_ge(rstd_ok, n + 1)
                if n >= 2:
                    v.wait_ge(q_split, n - 1)
                for t in range(HH * n, HH * (n + 1)):
                    nc.vector.tensor_scalar(xn[:, t % NH, :], x_sb[:, t, :], mv[:, t, 0:1], rstd[:, t:t + 1],
                                            ALU.subtract, ALU.mult).then_inc(xn_ok, 1)

            def split_half(n):
                at = slice(HH * (n % 2), HH * (n % 2 + 1))
                part = q_parts[n]
                v.wait_ge(xn_ok, HH * (n + 1))
                if n:
                    v.wait_ge(q_split, n)
                link(nc.vector.tensor_copy(part[:, 0], xn[:, at, :]))
                link(nc.vector.tensor_tensor(rest_v, xn[:, at, :], part[:, 0], ALU.subtract))
                link(nc.vector.tensor_copy(part[:, 1], rest_v))
                nc.vector.tensor_tensor(part[:, 2], rest_v, part[:, 1], ALU.subtract).then_inc(q_split, 1)

            nc.vector.memset(st[KS:KS + 32, :, 1].rearrange("p s h l -> p s (h l)").bitcast(u32), 0x3F803F80
                             ).then_inc(ones_set, 1)
            stats_half(0)
            normalise_half(0)
            stats_half(1)
            split_half(0)
            normalise_half(1)
            split_half(1)
            stats_half(2)
            stats_half(3)
            normalise_half(2)
            split_half(2)
            normalise_half(3)
            v.wait_ge(tanh_ok, 1)
            link(nc.vector.tensor_tensor(c_att[:], tanhs[:, 0:1], gates[:, 2:3], ALU.mult))

            def coefficients():
                v.wait_ge(scales_in, 48)
                nc.vector.tensor_scalar(ds_row[:], ds_row[:], tanhs[:, 1:2], None, ALU.mult)
                nc.vector.tensor_scalar(gs_half[:], gs[:], 0.5, None, ALU.mult).then_inc(coef_ok, 1)
                v.wait_ge(coef_ok, 1)
                link(nc.vector.tensor_tensor(gus[:], gs_half[:], us[:], ALU.mult))

            def reduce_max(i, k, off, h):
                r, s = rs(i, k, off)
                b = RING * r + s
                v.wait_ge(s_ok, NH * b + h + 1)
                if h == 0 and has(i, k, off - 2):
                    v.wait_ge(mx_split, b - 1)
                nc.vector.tensor_reduce(neg_max[:, s % 2, LT * h:LT * (h + 1)],
                                        ps[:, PS_S + h % NSB, :].rearrange("p (t l) -> p t l", t=LT),
                                        axis=AX.X, op=ALU.max, negate=True).then_inc(max_ok, 1)

            def split_max(i, k, off):
                r, s = rs(i, k, off)
                b = RING * r + s
                v.wait_ge(max_ok, NH * (b + 1))
                if not isinstance(b, int) or b > 0:
                    v.wait_ge(mt_ok, b)
                nc.vector.tensor_copy(max_parts[:, 0, :], neg_max[:, s % 2]).then_inc(mx_hi, 1)
                v.wait_ge(mx_hi, b + 1)
                nc.vector.tensor_tensor(max_parts[:, 1, :], neg_max[:, s % 2], max_parts[:, 0, :],
                                        ALU.subtract).then_inc(mx_split, 1)

            def copy_max(i, k, off):
                r, s = rs(i, k, off)
                v.wait_ge(mt_ok, RING * r + s + 1)
                if has(i, k, off - 1):
                    r1, s1 = rs(i, k, off - 1)
                    v.wait_ge(mx_in[s1], 16 * (r1 + 1))
                nc.vector.tensor_copy(max_t[:], ps[0:MAXROWS * NH * LT, PS_M, 0:P]).then_inc(mt_sb, 1)

            for h in range(NH):
                reduce_max(0, 0, 0, h)
            split_max(0, 0, 0)
            for h in range(NH):
                reduce_max(0, 0, 1, h)
                if h == 1:
                    copy_max(0, 0, 0)

            def binades(m, half):
                raw, exp = (a[:, bass.ds(m, 1), :].rearrange("p a n -> p (a n)") for a in (w_all, w_exp))
                for n in (WD,) if m is WD else range(WD):
                    v.wait_ge(w_in[n], 16)
                if not half:
                    nc.vector.tensor_scalar(exp.bitcast(u32), raw.bitcast(u32), 0x7F800000, None,
                                            ALU.bitwise_and).then_inc(w_and, 1)
                else:
                    v.wait_ge(w_and, m + 1)
                    nc.vector.tensor_scalar(exp, exp, E4M3_MIN_EXP, E4M3_MAGIC,
                                            ALU.max, ALU.mult).then_inc(w_exp_ok, 1)

            def reciprocals(g):
                v.wait_ge(sum_in[g], 32)
                if g:
                    v.wait_ge(rec_out[g - 1], 32)
                nc.vector.reciprocal(r_sp[:], s_sp[:]).then_inc(rec_ok, 1)

            def add_attention(c, g):
                v.wait_ge(att_ok, c + 1)
                u = u_n[:, bass.ds(HH * (c - 2 * g), HH), :].rearrange("p h l -> p (h l)")
                xh = x_sb[:, bass.ds(HH * c, HH), :].rearrange("p h l -> p (h l)")
                nc.vector.scalar_tensor_tensor(xh, u, c_att[:, 0:1], xh, ALU.mult, ALU.add).then_inc(x1_ok, 1)

            def norm_stats(c, tiles):
                v.wait_ge(x1_ok, c + 1)
                if not isinstance(c, int):
                    apart(v)
                for q in tiles:
                    nc.vector.bn_stats(stats[:, q, :], x_sb[:, bass.ds(CH * c + q, 1), :].rearrange("p a l -> p (a l)")
                                       ).then_inc(n2_stats, 1)

            def norm_aggr(c):
                for q in range(CH):
                    v.wait_ge(n2_stats, CH * c + q + 1)
                    apart(v)
                    nc.vector.bn_aggr(mv[:, q, :], stats[:, q, :]).then_inc(n2_aggr, 1)
                v.wait_ge(n2_aggr, CH * c + CH)
                nc.vector.tensor_scalar(veps[:, bass.ds(CH * c, CH)], mv[:, 0:CH, 1], EPS, None,
                                        ALU.add).then_inc(v2_ok, CH)

            def norm_chunk(c):
                norm_stats(c, range(CH))
                norm_aggr(c)

            def norm_apply(c):
                v.wait_ge(r2_ok, c + 1)
                if not isinstance(c, int) or c > 0:
                    v.wait_ge(t_ok, c)
                for q in range(CH):
                    t = CH * c + q
                    nc.vector.tensor_scalar(xn2[:, q, :], x_sb[:, bass.ds(t, 1), :].rearrange("p a l -> p (a l)"),
                                            mv[:, q, 0:1], rstd[:, bass.ds(t, 1)],
                                            ALU.subtract, ALU.mult).then_inc(n2_ok, 1)

            def chunk_low(c, bank=PS_T):
                v.wait_ge(hi_ok, c + 1)
                hi, lo = (x_t[:, bass.ds(c, 1), part].rearrange("p c t n -> p (c t) n") for part in range(2))
                nc.vector.tensor_tensor(lo, ps[:, bank:bank + HT, :], hi, ALU.subtract).then_inc(lo_ok, 1)

            def step(i, k):
                if has(i, k, 1):
                    split_max(i, k, 1)
                for h in range(NH):
                    if has(i, k, 2):
                        reduce_max(i, k, 2, h)
                    if h == 1 and has(i, k, 1):
                        copy_max(i, k, 1)
                    if h == 1 and not isinstance(i, int) and k < 2:
                        binades(i - 1, k)
                    if final(i) and k == 0 and h == 1:
                        binades(WD, 0)
                    if final(i) and k == 0 and h == 4:
                        binades(WD, 1)
                if final(i) and k == 0:
                    reciprocals(0)
                if final(i) and k == 1:
                    coefficients()
                if final(i) and k == 2:
                    add_attention(0, 0)
                    norm_chunk(0)
                    norm_apply(0)
                if final(i) and k == 3:
                    add_attention(1, 0)
                    chunk_low(0, PS_T0)
                    norm_chunk(1)

            steps(v, step)

            def scale_out(c):
                v.wait_ge(y_ok, c + 1)
                if isinstance(c, int):
                    v.wait_ge(o_ok, c - NBUF + 1)
                scale = ds_row[:].rearrange("p (a b l) -> p a b l", a=1, b=1).broadcast_to([P, 2, 2, L])
                nc.vector.tensor_tensor(buffer(yo, c).rearrange("p (a b l) -> p a b l", a=2, b=2),
                                        ps[:, PS_Y:PS_Y + 2, :].rearrange("p a (b l) -> p a b l", b=2),
                                        scale, ALU.mult).then_inc(yo_ok, 1)

            def chunk(c, start, last):
                for it in range(IT):
                    n = IT * c + it
                    v.wait_ge(th_ok, n + 1)
                    nc.vector.scalar_tensor_tensor(ga[:, it % 2, :], th[:, it % 2, :], 1.0,
                                                   ps[:, PS_GU + 2 * (it % 2), :], ALU.add, ALU.mult).then_inc(ga_ok, 1)
                    v.wait_ge(ga_ok, n + 1)
                    if it >= 2 or not start:
                        v.wait_ge(fl_ok, n - 1)
                    nc.vector.scalar_tensor_tensor(fu[:, it % 2, :], ps[:, PS_GU + 2 * (it % 2) + 1, :],
                                                   gus[:, it:it + 1], ga[:, it % 2, :],
                                                   ALU.mult, ALU.mult).then_inc(fu_ok, 1)
                    if it == 0 and not start and not last:
                        add_attention(c + 1, 1)
                        norm_stats(c + 1, range(CH // 2))
                    if it == 1 and not start and not last:
                        norm_stats(c + 1, range(CH // 2, CH))
                        norm_aggr(c + 1)
                    if start and it == 1:
                        reciprocals(1)
                    if it == 1 and not start:
                        scale_out(c - 1)
                    if it == 3 and last:
                        v.wait_ge(yo_ok, c)
                        v.wait_ge(out_ok, 16 * CH * (c - 1))
                        x1 = x_sb[:, CH * (c - 1):CH * c, :].rearrange("p h l -> p (h l)")
                        nc.vector.tensor_tensor(buffer(o_sb, c - 1), buffer(yo, c - 1), x1,
                                                ALU.add).then_inc(last_ok, 1)
                    if it == (2 if start else 3) and not last:
                        norm_apply(c + 1)
                    if it == 4 and not last:
                        chunk_low(c + 1)

            chunk(0, True, False)
            with v.Fori(1, NCH - 1) as c:
                chunk(c, False, False)
            chunk(NCH - 1, False, True)
            v.wait_ge(fh_ok, IT * NCH)
            nc.vector.tensor_tensor(f_lo[:, IT - 1, :], fu[:, (IT - 1) % 2, :], f_hi[:, IT - 1, :].bitcast(f32),
                                    ALU.subtract).then_inc(fl_last, 1)
            v.wait_ge(o_ok, NCH - NBUF)
            for n in range(2):
                half = slice(2 * L * n, 2 * L * (n + 1))
                y, o = buffer(yo, NCH - 1)[:, half], buffer(o_sb, NCH - 1)[:, half]
                v.wait_ge(y_ok, NCH + n)
                nc.vector.tensor_tensor(y.rearrange("p (b l) -> p b l", b=2),
                                        ps[:, PS_Y + n, :].rearrange("p (b l) -> p b l", b=2),
                                        ds_row[:].rearrange("p (b l) -> p b l", b=1).broadcast_to([P, 2, L]),
                                        ALU.mult).then_inc(yo_ok, 1)
                v.wait_ge(yo_ok, NCH + n)
                t = CH * (NCH - 1) + 2 * n
                nc.vector.tensor_tensor(o, y, x_sb[:, t:t + 2, :].rearrange("p h l -> p (h l)"),
                                        ALU.add).then_inc(last_ok, 1)

        @block.tensor
        def _(pe):
            def scores(r, s, h):
                b = RING * r + s
                if not isinstance(b, int) or b > 0 or h >= NSB:
                    pe.wait_ge(max_ok, NH * b + h - NSB + 1)
                for t in range(LT):
                    last = nc.tensor.matmul(ps[:, PS_S + h % NSB, L * t:L * (t + 1)],
                                            q_st[0:KS, s, h, P * t:P * (t + 1)], k_st[0:KS, s, h, :],
                                            start=True, stop=True)
                last.then_inc(s_ok, 1)

            def scores_t(i, k, h):
                b = RING * i + k
                if h == 0:
                    pe.wait_ge(mx_in[k], 16 * (i + 1))
                if h >= NTB or has(i, k, -1):
                    pe.wait_ge(exp_ok, NH * b + h - NTB + 1)
                for t in range(LT):
                    last = nc.tensor.matmul(ps[:, PS_ST + h % NTB, L * t:L * (t + 1)],
                                            k_st[0:KS + MAXROWS, k, h, P * t:P * (t + 1)],
                                            q_st[0:KS + MAXROWS, k, h, :], start=True, stop=True)
                last.then_inc(st_ok, 1)

            def transpose_max(i, k, off):
                r, s = rs(i, k, off)
                b = RING * r + s
                pe.wait_ge(mx_split, b + 1)
                pe.wait_ge(vt_sb, b if has(i, k, off - 1) else 1)
                nc.tensor.matmul(ps[0:MAXROWS * NH * LT, PS_M, 0:P], max_parts[:].rearrange("p a n -> p (a n)"),
                                 ident_b[:], start=True, stop=True).then_inc(mt_ok, 1)

            def transpose_ctx(i, k, off):
                r, s = rs(i, k, off)
                b = RING * r + s
                pe.wait_ge(ctx_in[s], 16 * (r + 1))
                if has(i, k, off - 1):
                    pe.wait_ge(mt_sb, b + 1)
                for t in range(LT):
                    last = nc.tensor.transpose(ps[:, PS_M, P * t:P * (t + 1)], ctx_t[:, s, P * t:P * (t + 1)], ident[:])
                last.then_inc(vt_ok, 1)

            def weighted(i, k, off, quad, t):
                r, s = rs(i, k, off)
                b = RING * r + s
                if t == 0:
                    pe.wait_ge(exp_ok, NH * b + QUAD * (quad + 1))
                    if quad == 0:
                        pe.wait_ge(vt_sb, b + 1)
                        if has(i, k, off - 1):
                            pe.wait_ge(u_ok, b)
                for j in range(QUAD):
                    h = QUAD * quad + j
                    last = nc.tensor.matmul(ps[32 * j:32 * (j + 1), PS_U, L * quad:L * (quad + 1)],
                                            v_t[:, s % 2, t, h, :], p_t[:, s % 2, h, L * t:L * (t + 1)],
                                            start=(t == 0), stop=(t == LT - 1))
                if quad == 1 and t == LT - 1:
                    last.then_inc(pv_ok, 1)

            def transposes(c, bank=PS_T):
                pe.wait_ge(n2_ok, CH * (c + 1))
                for q in range(CH):
                    for ht in range(HT):
                        last = nc.tensor.transpose(ps[:, bank + ht, P * q:P * (q + 1)],
                                                   xn2[:, q, P * ht:P * (ht + 1)], ident[:])
                last.then_inc(t_ok, 1)

            pe.wait_ge(consts, 5)
            transpose_ctx(0, 0, 0)
            pe.wait_ge(q_in[0], STACK)
            pe.wait_ge(k_first[0], STACK)
            for h in range(NH):
                scores(0, 0, h)
            pe.wait_ge(q_in[1], STACK)
            pe.wait_ge(k_first[1], STACK)
            for h in range(NH):
                scores(0, 1, h)
                if h == QUAD - 1:
                    transpose_max(0, 0, 0)
            pe.wait_ge(ones_set, 1)

            def step(i, k):
                b = RING * i + k
                for h in range(NH):
                    if has(i, k, 0):
                        scores_t(i, k, h)
                    if final(i) and k == RING - 1 and h == 7:
                        pe.wait_ge(max_ok, NH * NB)
                        transposes(0, PS_T0)
                    if has(i, k, 2):
                        r, s = rs(i, k, 2)
                        if h == 0:
                            pe.wait_ge(q_in[s], STACK * (r + 1))
                            pe.wait_ge(k_in[s], STACK * (r if s < 2 else r + 1))
                        scores(r, s, h)
                    if h == 2 and has(i, k, 1):
                        transpose_max(i, k, 1)
                    if h in (1, 2) and has(i, k, -1):
                        weighted(i, k, -1, 1, h - 1)
                    if h == 6 and has(i, k, 1):
                        transpose_ctx(i, k, 1)
                    if h in (5, 6) and has(i, k, 0):
                        weighted(i, k, 0, 0, h - 5)

            steps(pe, step)

            def gate_up(c, it, start):
                n = IT * c + it
                if it == 0:
                    pe.wait_ge(lo_ok, c + 1)
                if it >= 2 or not start:
                    pe.wait_ge(fu_ok, n - 1)
                for m, w in enumerate((wg, wu)):
                    for j in range(2 * HT):
                        ht, part = j // 2, j % 2
                        last = nc.tensor.matmul(ps[:, PS_GU + 2 * (it % 2) + m, :], w[:, ht, P * it:P * (it + 1)],
                                                x_t[:, bass.ds(c, 1), part, ht, :].rearrange("p c n -> p (c n)"),
                                                start=(j == 0), stop=(j == 2 * HT - 1))
                last.then_inc(gu_ok, 1)

            def down(c, it):
                if c is NCH - 1 and it == IT - 1:
                    pe.wait_ge(fl_last, 1)
                else:
                    pe.wait_ge(fl_ok, IT * c + it + 1)
                if it == 0 and (not isinstance(c, int) or c > 0):
                    pe.wait_ge(yo_ok, c)
                if it == 0:
                    for n in range(CH // 2):
                        nc.tensor.matmul(ps[:, PS_Y + n, :], zeros[:, 0:P], zeros[:], start=True, stop=False)
                for q in range(CH):
                    for part, f in enumerate((f_hi, f_lo)):
                        last = nc.tensor.matmul(ps[:, PS_Y + q // 2, L * (q % 2):L * (q % 2 + 1)],
                                                f[:, it, P * q:P * (q + 1)], wd[:, it, :],
                                                start=False, stop=(it == IT - 1 and part == 1 and q % 2 == 1))
                    if c is NCH - 1 and it == IT - 1 and q == 1:
                        last.then_inc(y_ok, 1)
                if it == IT - 1:
                    last.then_inc(y_ok, 1)

            pe.wait_ge(w_ok, WD)

            def chunk(c, start, last):
                for it in range(IT):
                    gate_up(c, it, start)
                    if start and it == 2:
                        pe.wait_ge(u_ok, NB)
                        pe.wait_ge(mt_sb, NB)
                        pe.wait_ge(w_ok, WD + 1)
                    if it >= 3:
                        down(c, it - 3)
                    elif not start:
                        down(c - 1, it + 3)
                    if it == 4 and not last:
                        transposes(c + 1)

            chunk(0, True, False)
            with pe.Fori(1, NCH - 1) as c:
                chunk(c, False, False)
            chunk(NCH - 1, False, True)
            for it in range(3, IT):
                down(NCH - 1, it)


_INS = ["x", "ctx_2048", "g_xattn", "g_ffn", "L0_xattn_gamma", "L0_ffn_gate_w", "L0_ffn_up_w", "L0_ffn_down_w",
        "L0_ffn_gate_scale", "L0_ffn_up_scale", "L0_ffn_down_scale"]


def kernel(**inputs):
    import numpy as np
    import concourse.bacc as bacc
    from concourse import mybir
    from concourse.bass_utils import run_bass_kernel_spmd

    nc = bacc.Bacc("TRN2", target_bir_lowering=False, num_devices=1)
    arrays, args = {}, []
    for name in _INS:
        a = np.ascontiguousarray(inputs[name])
        if a.ndim == 0:
            a = a.reshape(1)
        arrays[f"in_{name}"] = a
        args.append(nc.dram_tensor(f"in_{name}", a.shape, mybir.dt.from_np(a.dtype), kind="ExternalInput").ap())
    shape = (NB, D, L)
    result = nc.dram_tensor("out_x", shape, mybir.dt.float32, kind="ExternalOutput").ap()
    build(nc, *args, result)
    r = run_bass_kernel_spmd(nc, [arrays], core_ids=[0])
    return r.results[0]["out_x"]
```
